# Optimizing a Trainium2 kernel written in Bass

```python
import numpy as np
import jax
import jax.numpy as jnp

def _softmax(x, axis=-1):
    return jax.nn.softmax(x, axis=axis)

def _gelu(x):
    return jax.nn.gelu(x, approximate=True)

def _silu(x):
    return jax.nn.silu(x)

def _sigmoid(x):
    return jax.nn.sigmoid(x)

def _layernorm(x, axis=-1, eps=1e-05):
    m = jnp.mean(x, axis=axis, keepdims=True)
    v = jnp.var(x, axis=axis, keepdims=True)
    return (x - m) / jnp.sqrt(v + eps)

def _scatter_add(tgt, idx, src, axis=0):
    return tgt.at[idx].add(src)

def _segment_sum(src, seg, n):
    return jax.ops.segment_sum(src, seg, n)
kernel_name = 'mk_gnn_resnorm_d2_gnn_r64_18499d'

def setup_inputs(seed: int=0):
    np.random.seed(seed)
    _w = jnp.asarray

    def _rec_inputs():
        import jax
        import jax.numpy as jnp
        _gk = jax.random.key(seed)
        x = -0.000202 + 1 * jax.random.normal(jax.random.fold_in(_gk, 1), (50000, 128), jnp.float32)
        src = jax.random.randint(jax.random.fold_in(_gk, 2), (12500,), 0, 50000, jnp.int32)
        dst = jnp.minimum((50000 * jax.random.uniform(jax.random.fold_in(_gk, 3), (12500,)) ** 2.0).astype(jnp.int32), 49999)
        _o = jnp.argsort(dst, stable=True)
        src = src[_o]
        dst = dst[_o]
        edge_type_16 = jax.random.randint(jax.random.fold_in(_gk, 12), (12500,), 0, 16, jnp.int32)
        edge_weight = jax.random.uniform(jax.random.fold_in(_gk, 13), (12500,), jnp.float32, 0.0, 0.999998)
        return (x, src, dst, edge_type_16, edge_weight)
    x, src, dst, edge_type_16, edge_weight = _rec_inputs()

    def _L0_gnn_setup():
        import jax, jax.numpy as jnp
        import numpy as np
        N = 50000
        E = 9375
        C_IN = 128
        C_OUT = 128
        LN_EPS = 1e-05

        def layer_norm(h, gamma, beta):
            mu = jnp.mean(h, axis=-1, keepdims=True)
            var = jnp.var(h, axis=-1, keepdims=True)
            return (h - mu) * jax.lax.rsqrt(var + LN_EPS) * gamma + beta
        key = jax.random.key(seed)
        ks = jax.random.split(key, 8)
        x = jax.random.normal(ks[0], (N, C_IN), dtype=jnp.float32)
        edge_index = jax.random.randint(ks[1], (2, E), 0, N, dtype=jnp.int64)
        edge_weight = jax.random.uniform(ks[2], (E,), dtype=jnp.float32)
        lim1 = 1.0 / np.sqrt(C_IN)
        pool_w = jax.random.uniform(ks[3], (C_IN, C_IN), minval=-lim1, maxval=lim1, dtype=jnp.float32)
        pool_b = jax.random.uniform(ks[4], (C_IN,), minval=-lim1, maxval=lim1, dtype=jnp.float32)
        lim2 = 1.0 / np.sqrt(2 * C_IN)
        final_w = jax.random.uniform(ks[5], (2 * C_IN, C_OUT), minval=-lim2, maxval=lim2, dtype=jnp.float32)
        final_b = jax.random.uniform(ks[6], (C_OUT,), minval=-lim2, maxval=lim2, dtype=jnp.float32)
        return {'x': x, 'edge_index': edge_index, 'edge_weight': edge_weight, 'pool_w': pool_w, 'pool_b': pool_b, 'ln_pool_g': jnp.ones((C_IN,), jnp.float32), 'ln_pool_b': jnp.zeros((C_IN,), jnp.float32), 'final_w': final_w, 'final_b': final_b, 'ln_final_g': jnp.ones((C_OUT,), jnp.float32), 'ln_final_b': jnp.zeros((C_OUT,), jnp.float32), 'coeff_raw': jnp.float32(0.5)}
    _L0_gnn_all = _L0_gnn_setup()
    _L0_gnn_in = {k: v for k, v in _L0_gnn_all.items() if k in ('pool_w', 'pool_b', 'ln_pool_g', 'ln_pool_b', 'final_w', 'final_b', 'ln_final_g', 'ln_final_b', 'coeff_raw')}
    del _L0_gnn_all

    def _L1_gnn_setup():
        import jax, jax.numpy as jnp
        import numpy as np
        N = 100000
        E = 25000
        IN_CH = 128
        OUT_CH = 128
        NUM_REL = 16
        NUM_BASES = 8
        key = jax.random.key(seed)
        k1, k2, k3, k4, k5, k6 = jax.random.split(key, 6)
        x = jax.random.normal(k1, (N, IN_CH), dtype=jnp.float32)
        edge_index = jax.random.randint(k2, (2, E), 0, N, dtype=jnp.int64)
        edge_type = jax.random.randint(k3, (E,), 0, NUM_REL, dtype=jnp.int64)
        wscale = np.sqrt(6.0 / (IN_CH + OUT_CH)).astype(np.float32)
        weight = jax.random.uniform(k4, (NUM_BASES + 1, IN_CH, OUT_CH), dtype=jnp.float32, minval=-wscale, maxval=wscale)
        cscale = np.sqrt(6.0 / (NUM_REL + NUM_BASES)).astype(np.float32)
        comp = jax.random.uniform(k5, (NUM_REL, NUM_BASES), dtype=jnp.float32, minval=-cscale, maxval=cscale)
        bias = jnp.zeros((OUT_CH,), dtype=jnp.float32)
        return {'x': x, 'weight': weight, 'comp': comp, 'bias': bias, 'edge_index': edge_index, 'edge_type': edge_type, 'num_nodes': N}
    _L1_gnn_all = _L1_gnn_setup()
    _L1_gnn_in = {k: v for k, v in _L1_gnn_all.items() if k in ('weight', 'comp', 'bias')}
    del _L1_gnn_all
    return {'x': x, 'src': src, 'dst': dst, 'edge_type_16': edge_type_16, 'edge_weight': edge_weight, 'L0_gnn_pool_w': _L0_gnn_in['pool_w'], 'L0_gnn_pool_b': _L0_gnn_in['pool_b'], 'L0_gnn_ln_pool_g': _L0_gnn_in['ln_pool_g'], 'L0_gnn_ln_pool_b': _L0_gnn_in['ln_pool_b'], 'L0_gnn_final_w': _L0_gnn_in['final_w'], 'L0_gnn_final_b': _L0_gnn_in['final_b'], 'L0_gnn_ln_final_g': _L0_gnn_in['ln_final_g'], 'L0_gnn_ln_final_b': _L0_gnn_in['ln_final_b'], 'L0_gnn_coeff_raw': _L0_gnn_in['coeff_raw'], 'L1_gnn_weight': _L1_gnn_in['weight'], 'L1_gnn_comp': _L1_gnn_in['comp'], 'L1_gnn_bias': _L1_gnn_in['bias']}

def reference(x, src, dst, edge_type_16, edge_weight, L0_gnn_pool_w, L0_gnn_pool_b, L0_gnn_ln_pool_g, L0_gnn_ln_pool_b, L0_gnn_final_w, L0_gnn_final_b, L0_gnn_ln_final_g, L0_gnn_ln_final_b, L0_gnn_coeff_raw, L1_gnn_weight, L1_gnn_comp, L1_gnn_bias):
    import jax
    import jax.numpy as jnp

    def _L0_gnn_ref(x, edge_index, edge_weight, pool_w, pool_b, ln_pool_g, ln_pool_b, final_w, final_b, ln_final_g, ln_final_b, coeff_raw):
        import jax, jax.numpy as jnp
        import numpy as np
        N = 50000
        E = 9375
        C_IN = 128
        C_OUT = 128
        LN_EPS = 1e-05

        def layer_norm(h, gamma, beta):
            mu = jnp.mean(h, axis=-1, keepdims=True)
            var = jnp.var(h, axis=-1, keepdims=True)
            return (h - mu) * jax.lax.rsqrt(var + LN_EPS) * gamma + beta
        src, dst = (edge_index[0], edge_index[1])
        coeff = jax.nn.softplus(coeff_raw)
        edge_features = x[src] * (1.0 + coeff * edge_weight[:, None])
        pooled = edge_features @ pool_w + pool_b
        pooled = jax.nn.relu(layer_norm(pooled, ln_pool_g, ln_pool_b))
        aggregate = jax.ops.segment_max(pooled, dst, num_segments=x.shape[0])
        aggregate = jnp.maximum(aggregate, 0.0)
        h = jnp.concatenate([x, aggregate], axis=-1)
        h = h @ final_w + final_b
        return jax.nn.relu(layer_norm(h, ln_final_g, ln_final_b))

    def _L1_gnn_ref(x, weight, comp, bias, edge_index, edge_type, num_nodes):
        import jax, jax.numpy as jnp
        import numpy as np
        N = 100000
        E = 25000
        IN_CH = 128
        OUT_CH = 128
        NUM_REL = 16
        NUM_BASES = 8
        'RGCN with basis decomposition, mean aggregation, root weight + bias.\n\n            agg[i, b, :] = (1/deg(i)) * sum_{e: dst(e)=i} comp[etype(e), b] * x[src(e)]\n            out = concat_b(agg, x_root) @ weight.reshape(-1, out_ch) + bias\n            '
        src = edge_index[0]
        dst = edge_index[1]
        num_bases = comp.shape[1]
        coeff = comp[edge_type]
        msg = x[src]
        aggs = [jax.ops.segment_sum(msg * coeff[:, b:b + 1], dst, num_segments=num_nodes) for b in range(num_bases)]
        agg = jnp.stack(aggs, axis=1)
        deg = jax.ops.segment_sum(jnp.ones((src.shape[0],), dtype=x.dtype), dst, num_segments=num_nodes)
        agg = agg / jnp.maximum(deg, 1.0)[:, None, None]
        feat = jnp.concatenate([agg.reshape(num_nodes, -1), x], axis=1)
        out = feat @ weight.reshape(-1, weight.shape[-1]) + bias
        return out
    edge_index = jnp.stack([src, dst])
    x = _layernorm(x + _L0_gnn_ref(x, edge_index, edge_weight, L0_gnn_pool_w, L0_gnn_pool_b, L0_gnn_ln_pool_g, L0_gnn_ln_pool_b, L0_gnn_final_w, L0_gnn_final_b, L0_gnn_ln_final_g, L0_gnn_ln_final_b, L0_gnn_coeff_raw), axis=-1)
    x = _layernorm(x + _L1_gnn_ref(x, L1_gnn_weight, L1_gnn_comp, L1_gnn_bias, edge_index, edge_type_16, 50000), axis=-1)
    return x

_drawn_inputs = setup_inputs


def setup_inputs(seed=0):
    import zlib

    import numpy as np

    out = dict(_drawn_inputs(seed))
    spreads = {'L0_gnn_ln_pool_g': (1.0, 0.2),
     'L0_gnn_ln_pool_b': (0.0, 0.62),
     'L0_gnn_ln_final_g': (1.0, 0.2),
     'L0_gnn_ln_final_b': (0.0, 0.1),
     'L1_gnn_bias': (0.0, 0.1)}
    factors = {'edge_weight': 8.0, 'L0_gnn_pool_b': 5.554}
    for name, (base, spread) in spreads.items():
        noise = np.random.default_rng([zlib.crc32(name.encode()), seed]).standard_normal(out[name].shape)
        drawn = base * np.exp(spread * noise) if base else spread * noise
        out[name] = jnp.asarray(drawn.astype(out[name].dtype))
    for name, factor in factors.items():
        out[name] = (out[name] * factor).astype(out[name].dtype)
    return out
```

```python
from contextlib import ExitStack

import concourse.bass as bass
from concourse import mybir

P = 128
CH = 4
DST, SRC = CH, CH + 1
NB = 8
REL = 16
PARTS = 3
LN_EPS = 1e-5
SKIP = 1 << 20
SLOTS = 4

ALU = mybir.AluOpType
ACT = mybir.ActivationFunctionType
F32 = mybir.dt.float32
BF16 = mybir.dt.bfloat16
I32 = mybir.dt.int32
U32 = mybir.dt.uint32
U8 = mybir.dt.uint8
AX_X = mybir.AxisListType.X


def need(eng, sem, count):
    if isinstance(count, int) and count <= 0:
        return
    eng.wait_ge(sem, count)


class Chain:

    def __init__(self, eng, sem):
        self.eng, self.sem, self.count, self.base = eng, sem, 0, 0

    def mark(self, ins):
        ins.then_inc(self.sem, 1)
        self.count += 1
        return self.count

    def need(self, at):
        self.eng.wait_ge(self.sem, self.base + at)

    def link(self, ins):
        self.need(self.mark(ins))


def run_steps(eng, first, loop_first, loops, last, step, chain=None):
    for s in range(first, loop_first):
        step(0, s)
    with eng.Fori(0, loops) as i:
        if chain:
            before = chain.count
            chain.base = i * chain.per_loop
        for c in range(loop_first, loop_first + SLOTS):
            step(i, c)
        if chain:
            assert chain.count - before == chain.per_loop, (chain.count - before)
    if chain:
        chain.base = (loops - 1) * chain.per_loop
    for s in range(loop_first + SLOTS * loops, last + 1):
        step(0, s)


def gnn_kernel(nc, x, src_cols, dst_cols, dst_next_cols, dst_line, type_line, weight_cols,
               pool_w, pool_b, ln_pool_g, ln_pool_b, final_w, final_b, ln_final_g, ln_final_b,
               coeff_raw, weight, comp, bias, out):
    N, D = x.shape
    TILES = src_cols.shape[1]
    EP = TILES * P
    ROWS = CH * P
    GROUPS = -(-N // ROWS)
    TAIL = (N - (GROUPS - 1) * ROWS) // CH
    assert GROUPS == TILES and D == P and (N - (GROUPS - 1) * ROWS) % CH == 0

    LOOP0 = 2 * SLOTS
    LOOPS = (TILES - 2 - LOOP0) // SLOTS
    LAST_A = TILES + 3
    LAST_C = TILES + 2

    x1_table = nc.dram_tensor("x1_table", [N, D], F32).ap()

    with ExitStack() as ctx:
        def sb(name, shape, dt=F32):
            return ctx.enter_context(nc.sbuf_tensor(name, shape, dt))

        def sem(name):
            return ctx.enter_context(nc.semaphore(name))

        ident = sb("ident", [P, P])
        zero = sb("zero", [P, P])
        part_id = sb("part_id", [P, 1])
        w_raw = sb("w_raw", [P, 12, D])
        row_mean = sb("row_mean", [P, 16])
        w_cen = sb("w_cen", [P, 12, D])
        vec_raw = sb("vec_raw", [P, 7, D])
        vec_cen = sb("vec_cen", [P, 3, D])
        split = sb("split", [P, PARTS, 2 * D], BF16)
        rest = sb("rest", [P, 2, 2 * D])
        bias3 = sb("bias3", [PARTS, 2, CH * D], BF16)
        ones3 = sb("ones3", [PARTS, P], BF16)
        comp_raw = sb("comp_raw", [PARTS * REL, NB])
        comp_split = sb("comp_split", [PARTS * REL, PARTS, NB], BF16)
        comp_rest = sb("comp_rest", [PARTS * REL, 2, NB])
        comp_sel = sb("comp_sel", [PARTS * REL, NB], BF16)
        comp_rep = sb("comp_rep", [PARTS * REL, NB, P], BF16)
        part_mask = sb("part_mask", [P, 2, PARTS])
        rel_id = sb("rel_id", [PARTS * REL, 1])
        one = sb("one", [P, 1])
        soft = sb("soft", [P, 6])
        src_i = sb("src_i", [P, TILES], I32)
        dst_i = sb("dst_i", [P, TILES], I32)
        dst_n = sb("dst_n", [P, TILES], I32)
        scat_i = sb("scat_i", [P, TILES], I32)
        pair_a = sb("pair_a", [P, TILES + 2, 2], I32)
        pair_c = sb("pair_c", [P, TILES + 5, 2], I32)
        idx = sb("idx", [P, SLOTS, 2], I32)
        same_next = sb("same_next", [P, TILES])
        e_scale = sb("e_scale", [P, TILES])
        e_weight = sb("e_weight", [P, TILES])
        inv_deg = sb("inv_deg", [P, TILES])
        same_prev = sb("same_prev", [P, EP], U8)
        onehot = sb("onehot", [PARTS * REL, EP], BF16)
        rows = sb("rows", [P, SLOTS, CH + 2, D])
        xT = sb("xT", [P, 2, CH + 2, D])
        hn = sb("hn", [P, 2, CH + 1, D])
        hp = sb("hp", [P, D])
        pooled = sb("pooled", [P, 2, D])
        work = sb("work", [P, 4 * (CH + 1), D])
        x1 = work[:, 0:2 * (CH + 1), :].rearrange("p (b c) d -> p b c d", b=2)
        x1T = work[:, 2 * (CH + 1):, :].rearrange("p (b c) d -> p b c d", b=2)
        aggT = sb("aggT", [P, 2, D])
        outb = sb("outb", [P, 2, CH, D])
        bn = sb("bn", [P, 3, CH + 2, 6])
        st = sb("st", [P, 3, 8, CH + 2])
        x1_dst = sb("x1_dst", [P, TILES, D])
        y_root = sb("y_root", [P, TILES * D + P])

        line = y_root[:, :].bitcast(I32)
        types = x1_dst[:, :, :].rearrange("p t d -> p (t d)").bitcast(I32)
        pos = x1_dst[:, :, :].rearrange("p t d -> p (t d)")

        prod = work[:, 0:2 * NB, :].rearrange("p (b m) d -> p b m d", b=2)

        ps = ctx.enter_context(nc.psum_tensor("ps", [P, 4, 1024], F32))
        XT, H, VT, Y = (ps[:, r, :] for r in range(4))
        CB = [ps[:, 0, :], ps[:, 1, :]]
        GT = [ps[:, 2, 0:P], ps[:, 2, 512:512 + P]]
        MT, ST = ps[:, 3, 0:P], ps[:, 3, 512:512 + P]

        names = ("weights_in", "edges_in", "line_in", "types_in", "const_ready", "ident_ready", 
                 "setup_dve", "soft_dve", "soft_act", "pos_ready", "pos_cols",
                 "pe_xt", "act_xt", "pe_h", "dve_t", "pool_b", "pool_p", "dve_x1", "pe_vt", "act_vt",
                 "dve_scan", "pe_y", "dve_r3", "act_out", "pool_xd", "dve_q1", "dve_q2", "act_s1", "act_s2", "act_own", "dve_own", "pool_own", "idx_ready", "scat_ready",
                 "c_own", "pe_gt", "act_gt", "pe_cb", "dve_prod", "pe_mt", "dve_sum", "pe_st", "dve_rc", "dve_move",
                 "act_oc")
        S = {n: sem(n) for n in names}
        dense_in = [sem(f"dense_in{j}") for j in range(SLOTS)]
        dst_in = [sem(f"dst_in{j}") for j in range(SLOTS)]
        src_in = [sem(f"src_in{j}") for j in range(SLOTS)]
        x1_stored = [sem(f"x1_stored{j}") for j in range(2)]
        out_stored = [sem(f"out_stored{j}") for j in range(2)]
        x1_scattered = [sem(f"x1_scattered{j}") for j in range(SLOTS)]
        x1_in = [sem(f"x1_in{j}") for j in range(SLOTS)]
        out_scattered = [sem(f"out_scattered{j}") for j in range(SLOTS)]

        full = (GROUPS - 1) * ROWS
        x_groups = x[0:full, :].rearrange("(g p c) d -> g p (c d)", p=P, c=CH)
        x1_groups = x1_table[0:full, :].rearrange("(g p c) d -> g p (c d)", p=P, c=CH)
        out_groups = out[0:full, :].rearrange("(g p c) d -> g p (c d)", p=P, c=CH)
        x_tail = x[full:N, :].rearrange("(p c) d -> p (c d)", c=CH)
        x1_tail = x1_table[full:N, :].rearrange("(p c) d -> p (c d)", c=CH)
        out_tail = out[full:N, :].rearrange("(p c) d -> p (c d)", c=CH)

        W_TOP, W_BOT, W_POOL, W_BASE, W_ROOT = 0, 1, 2, 3, 11
        GAM_F, BET_F, GAM_P, BET_P = 3, 4, 5, 6
        N_W, N_EDGE = 7 + 4 + 1 + PARTS, 4

        def cols(s_lo, s_hi):
            return slice(s_lo * D, s_hi * D)

        def span(i, c, k_off):
            k = c - k_off
            if isinstance(i, int) and k < 0:
                return 0, 0
            lo = 0 if not isinstance(i, int) or k < GROUPS else CH
            hi = CH + 1 if not isinstance(i, int) or k > 0 else CH
            return lo, hi

        def ranges(i, c):
            lo, hi = span(i, c, 1)
            src = not isinstance(i, int) or c < TILES
            if src and hi == CH + 1:
                return [(lo, CH + 2)]
            return [(a, b) for a, b in ((lo, hi), (SRC, SRC + 1) if src else (0, 0)) if a < b]

        def halves(i, c, first):
            assert (c - first) % 2 == 0
            return 2 * i + (c - first) // 2

        def scatters_before(i, c):
            return i + (c - c % SLOTS) // SLOTS - (0 if c % SLOTS == 3 else 1)

        block = ctx.enter_context(nc.Block())

        @block.sync
        def _(sp):
            for w, ap in ((W_TOP, final_w[0:D, :]), (W_BOT, final_w[D:2 * D, :]), (W_POOL, pool_w)):
                sp.dma_start(w_raw[:, w, :], ap).then_inc(S["weights_in"], 16)
            sp.dma_start(w_raw[:, W_BASE:W_ROOT + 1, :], weight.rearrange("b k n -> k b n")) \
                .then_inc(S["weights_in"], 16)
            for v, ap in enumerate((final_b, bias, pool_b, ln_final_g, ln_final_b, ln_pool_g, ln_pool_b)):
                sp.dma_start(vec_raw[:, v, :], ap.broadcast_to([P, D])).then_inc(S["weights_in"], 16)
            sp.dma_start(soft[:, 0:1], coeff_raw.broadcast_to([P, 1])).then_inc(S["weights_in"], 16)
            for k in range(PARTS):
                sp.dma_start(comp_raw[k * REL:(k + 1) * REL, :], comp).then_inc(S["weights_in"], 16)
            for tile, ap in ((src_i, src_cols), (dst_i, dst_cols), (dst_n, dst_next_cols), (e_weight, weight_cols)):
                sp.dma_start(tile[:, :], ap).then_inc(S["edges_in"], 16)
            sp.dma_start(line[:, 0:EP + 1], dst_line.broadcast_to([P, EP + 1])).then_inc(S["line_in"], 16)
            sp.dma_start(types[0:PARTS * REL, :], type_line.broadcast_to([PARTS * REL, EP])) \
                .then_inc(S["types_in"], 16)

            def load(i, c):
                k = SLOTS * i + c - 1
                slot = c % SLOTS
                if not isinstance(k, int) or k < GROUPS - 1:
                    sp.dma_start(rows[:, slot, 0:CH, :].rearrange("p c d -> p (c d)"), x_groups[k]) \
                        .then_inc(dense_in[slot], 16)
                else:
                    sp.dma_start(rows[0:TAIL, slot, 0:CH, :].rearrange("p c d -> p (c d)"), x_tail) \
                        .then_inc(dense_in[slot], 16)

            sp.wait_ge(S["const_ready"], 5)
            load(0, 1)

            def step(i, c):
                s = SLOTS * i + c
                peeled = isinstance(s, int)
                if not peeled or s + 2 <= GROUPS:
                    need(sp, S["dve_x1"], s - 2)
                    load(i, c + 2)
                k = s - 2
                if not peeled or 0 <= k < GROUPS:
                    sp.wait_ge(S["dve_x1"], s - 1)
                    b = x1[:, c % 2, 0:CH, :].rearrange("p c d -> p (c d)")
                    if not peeled or k < GROUPS - 1:
                        sp.dma_start(x1_groups[k], b).then_inc(x1_stored[c % 2], 16)
                    else:
                        sp.dma_start(x1_tail, b[0:TAIL]).then_inc(x1_stored[c % 2], 16)
                k = s - 3
                if not peeled or 0 <= k < GROUPS:
                    sp.wait_ge(S["act_out"], s - 2)
                    b = outb[:, c % 2, :, :].rearrange("p c d -> p (c d)")
                    if not peeled or k < GROUPS - 1:
                        sp.dma_start(out_groups[k], b).then_inc(out_stored[c % 2], 16)
                    else:
                        sp.dma_start(out_tail, b[0:TAIL]).then_inc(out_stored[c % 2], 16)

            run_steps(sp, 0, LOOP0, LOOPS, LAST_A, step)

        @block.gpsimd
        def _(pool):
            pool.memset(zero[:, :], 0.0).then_inc(S["const_ready"], 1)
            pool.memset(one[:, :], 1.0).then_inc(S["const_ready"], 1)
            pool.memset(ones3[:, :], 1.0).then_inc(S["const_ready"], 1)
            pool.iota(part_id[:, :], [[0, 1]], base=0, channel_multiplier=1,
                      allow_small_or_imprecise_dtypes=True).then_inc(S["const_ready"], 1)
            pool.memset(rows[:, :, :, :], 0.0).then_inc(S["const_ready"], 1)
            pool.wait_ge(S["const_ready"], 5)
            pool.affine_select(out=ident[:, :], in_=zero[:, :], compare_op=ALU.not_equal, fill=1.0, base=0,
                               pattern=[[-1, P]], channel_multiplier=1).then_inc(S["ident_ready"], 1)
            pool.wait_ge(S["edges_in"], 16 * N_EDGE)
            pool.memset(pair_a[:, :, :], 0).then_inc(S["pool_own"], 1)
            pool.memset(pair_c[:, :, :], 0).then_inc(S["pool_own"], 1)
            pool.wait_ge(S["pool_own"], 2)
            pool.tensor_copy(pair_a[:, 0:TILES, 0], src_i[:, :]).then_inc(S["pool_own"], 1)
            pool.tensor_copy(pair_a[:, 2:TILES + 2, 1], dst_i[:, :]).then_inc(S["pool_own"], 1)
            pool.tensor_copy(pair_c[:, 0:TILES, 0], src_i[:, :]).then_inc(S["pool_own"], 1)
            pool.wait_ge(S["pool_own"], 5)
            pool.wait_ge(S["scat_ready"], 1)
            pool.tensor_copy(pair_c[:, 5:TILES + 5, 1], scat_i[:, :]).then_inc(S["pool_own"], 1)
            pool.wait_ge(S["pool_own"], 6)

            last_node = pool.to_reg(N - 1)

            def indirect(*args, **kw):
                pool.nop(nofuse=True)
                return pool.indirect_dma_start(*args, **kw)

            def fetch(table, u, slot, count):
                pool.tensor_copy(idx[:, slot:slot + 1, :], table[:, bass.ds(u, 1), :]).then_inc(S["idx_ready"], 1)
                pool.wait_ge(S["idx_ready"], count)

            def gather(i, c):
                t = SLOTS * i + c
                slot = c % SLOTS
                peeled = isinstance(t, int)
                fetch(pair_a, t, slot, t + 1)
                if not peeled or t < TILES:
                    indirect(
                        rows[:, slot, SRC, :], None, x[:, :],
                        bass.IndirectOffsetOnAxis(ap=idx[:, slot, 0:1].bitcast(U32), axis=0),
                        bounds_check=last_node, oob_is_err=False).then_inc(src_in[slot], 16)
                if not peeled or 0 <= t - 2 < TILES:
                    indirect(
                        rows[:, slot, DST, :], None, x[:, :],
                        bass.IndirectOffsetOnAxis(ap=idx[:, slot, 1:2].bitcast(U32), axis=0),
                        bounds_check=last_node, oob_is_err=False).then_inc(dst_in[slot], 16)

            gather(0, 0)
            gather(0, 1)

            def step(i, c):
                s = SLOTS * i + c
                peeled = isinstance(s, int)
                if not peeled or s + 2 < TILES + 2:
                    need(pool, S["dve_x1"], s - 2)
                    gather(i, c + 2)
                if not peeled or s <= TILES + 1:
                    lo, hi = span(i, c, 1)
                    pool.wait_ge(S["dve_t"], s + 1)
                    h = hn[:, c % 2, lo:hi, :]
                    if lo < hi:
                        pool.tensor_tensor(h, h, vec_raw[:, BET_F:BET_F + 1, :].broadcast_to([P, hi - lo, D]),
                                           ALU.add).then_inc(S["pool_b"], 1)
                    q = pooled[:, c % 2, :]
                    if not peeled or s < TILES:
                        pool.tensor_tensor(q, q, vec_raw[:, BET_P, :], ALU.add).then_inc(S["pool_p"], 1)
                if not peeled or 3 <= s <= TILES + 2:
                    pool.wait_ge(S["dve_x1"], s - 1)
                    pool.tensor_copy(x1_dst[:, bass.ds(s - 3, 1), :].rearrange("p t d -> p (t d)"),
                                     x1[:, c % 2, DST, :]).then_inc(S["pool_xd"], 1)

            run_steps(pool, 0, LOOP0, LOOPS, LAST_A, step)

            pool.wait_ge(S["pool_xd"], TILES)
            for j in range(2):
                pool.wait_ge(x1_stored[j], 16 * (GROUPS // 2))

            FETCHED_A, FETCHED_X = TILES + 2, TILES

            def scatter_x1(i, c):
                t = SLOTS * i + c
                slot = c % SLOTS
                pool.wait_ge(S["dve_move"], t + 1)
                fetch(pair_c, t + 5, slot, FETCHED_A + t + 1)
                indirect(
                    x1_table[:, :], bass.IndirectOffsetOnAxis(ap=idx[:, slot, 1:2].bitcast(U32), axis=0),
                    rows[:, slot, 0, :], None,
                    bounds_check=last_node, oob_is_err=False).then_inc(x1_scattered[slot], 16)

            run_steps(pool, 0, LOOP0, LOOPS, TILES - 1, scatter_x1)
            for j in range(SLOTS):
                pool.wait_ge(x1_scattered[j], 16 * len(range(j, TILES, SLOTS)))
            for j in range(2):
                pool.wait_ge(out_stored[j], 16 * (GROUPS // 2))

            def gather_x1(i, c):
                t = SLOTS * i + c
                slot = c % SLOTS
                if not isinstance(t, int) or t < TILES:
                    indirect(
                        rows[:, slot, 0, :], None, x1_table[:, :],
                        bass.IndirectOffsetOnAxis(ap=idx[:, slot, 0:1].bitcast(U32), axis=0),
                        bounds_check=last_node, oob_is_err=False).then_inc(x1_in[slot], 16)

            for c in range(2):
                fetch(pair_c, c, c, FETCHED_A + FETCHED_X + c + 1)
                gather_x1(0, c)

            def step_c(i, c):
                s = SLOTS * i + c
                peeled = isinstance(s, int)
                slot = (c + 2) % SLOTS
                need(pool, S["pe_gt"], s - 1 if not peeled else min(s - 1, TILES))
                need(pool, out_scattered[c % SLOTS], 16 * scatters_before(i, c))
                fetch(pair_c, s + 2, slot, FETCHED_A + FETCHED_X + s + 3)
                gather_x1(i, c + 2)
                if not peeled or 3 <= s:
                    pool.wait_ge(S["act_oc"], s - 2)
                    indirect(
                        out[:, :], bass.IndirectOffsetOnAxis(ap=idx[:, slot, 1:2].bitcast(U32), axis=0),
                        rows[:, c % SLOTS, 3, :], None,
                        bounds_check=last_node, oob_is_err=False).then_inc(out_scattered[c % SLOTS], 16)

            run_steps(pool, 0, LOOP0, LOOPS, LAST_C, step_c)
            for j in range(SLOTS):
                done = len([s for s in range(3, LAST_C + 1) if s % SLOTS == j])
                pool.wait_ge(out_scattered[j], 16 * done)

        @block.tensor
        def _(pe):
            pe.wait_ge(S["ident_ready"], 1)
            pe.wait_ge(S["const_ready"], 5)
            pe.wait_ge(S["pos_ready"], 1)
            for t in range(TILES):
                last = pe.matmul(H[:, t:t + 1], pos[0:1, t * P:(t + 1) * P], one[0:1, 0:1], start=True, stop=True)
            last.then_inc(S["pos_cols"], 1)
            pe.wait_ge(S["setup_dve"], 1)

            def step(i, c):
                s = SLOTS * i + c
                peeled = isinstance(s, int)
                slot, b = c % SLOTS, c % 2
                lo, hi = span(i, c, 1)
                if not peeled or s <= TILES + 1:
                    need(pe, S["act_xt"], s)
                    if lo < min(hi, CH):
                        pe.wait_ge(dense_in[slot], 16 * (i + (c - slot) // SLOTS + (1 if slot else 0)))
                    if hi == CH + 1:
                        pe.wait_ge(dst_in[slot], 16 * (i + (c - slot) // SLOTS + (1 if slot >= 2 else 0)))
                    if not peeled or s < TILES:
                        pe.wait_ge(src_in[slot], 16 * (i + (c - slot) // SLOTS + 1))
                    for m in (m for r in ranges(i, c) for m in range(*r)):
                        last = pe.transpose(XT[:, cols(m, m + 1)], rows[:, slot, m, :], ident[:, :])
                    last.then_inc(S["pe_xt"], 1)
                    pe.wait_ge(S["act_xt"], s + 1)
                    need(pe, S["dve_t"], s)
                    if lo < min(hi, CH):
                        pe.matmul(H[:, 0:CH * D], ones3[:, :], bias3[:, 0, :], start=True, stop=False,
                                  skip_group_check=True)
                        for m in range(CH):
                            last = pe.matmul(H[:, cols(m, m + 1)], xT[:, b, m, :], w_cen[:, W_TOP, :],
                                             start=False, stop=True, skip_group_check=True)
                    if hi == CH + 1:
                        pe.matmul(H[:, cols(DST, DST + 1)], ones3[:, :], bias3[:, 0, 0:D], start=True,
                                  stop=False, skip_group_check=True)
                        pe.matmul(H[:, cols(DST, DST + 1)], xT[:, b, DST, :], w_cen[:, W_TOP, :],
                                  start=False, stop=False, skip_group_check=True)
                        need(pe, S["dve_scan"], s - 1)
                        last = pe.matmul(H[:, cols(DST, DST + 1)], aggT[:, b, :], w_cen[:, W_BOT, :],
                                         start=False, stop=True, skip_group_check=True)
                    if not peeled or s < TILES:
                        last = pe.matmul(H[:, cols(SRC, SRC + 1)], xT[:, b, SRC, :], w_cen[:, W_POOL, :],
                                         start=(hi <= CH), stop=True, skip_group_check=True)
                    last.then_inc(S["pe_h"], 1)
                if not peeled or 1 <= s <= TILES + 2:
                    lo, hi = span(i, c, 2)
                    need(pe, S["act_vt"], s - 2)
                    need(pe, S["dve_scan"], min(s - 1, TILES) if peeled else s - 1)
                    if not peeled or s <= TILES:
                        pe.wait_ge(S["pool_p"], s)
                        last = pe.transpose(VT[:, cols(SRC, SRC + 1)], pooled[:, 1 - b, :], ident[:, :])
                    if not peeled or s >= 2:
                        pe.wait_ge(S["dve_x1"], s - 1)
                        for m in range(lo, hi):
                            last = pe.transpose(VT[:, cols(m, m + 1)], x1[:, b, m, :], ident[:, :])
                    last.then_inc(S["pe_vt"], 1)
                if not peeled or 2 <= s <= TILES + 2:
                    pe.wait_ge(S["act_vt"], s - 1)
                    need(pe, S["act_out"], s - 3)
                    if lo == 0:
                        pe.matmul(Y[:, 0:CH * D], ones3[:, :], bias3[:, 1, :], start=True, stop=False,
                                  skip_group_check=True)
                        for m in range(CH):
                            last = pe.matmul(Y[:, cols(m, m + 1)], x1T[:, b, m, :], w_cen[:, W_ROOT, :],
                                             start=False, stop=True, skip_group_check=True)
                    if hi == CH + 1:
                        pe.matmul(Y[:, cols(DST, DST + 1)], ones3[:, :], bias3[:, 1, 0:D], start=True,
                                  stop=False, skip_group_check=True)
                        last = pe.matmul(Y[:, cols(DST, DST + 1)], x1T[:, b, DST, :], w_cen[:, W_ROOT, :],
                                         start=False, stop=True, skip_group_check=True)
                    last.then_inc(S["pe_y"], 1)

            run_steps(pe, 0, LOOP0, LOOPS, LAST_A, step)

            pe.wait_ge(S["act_out"], TILES + 1)
            pe.wait_ge(S["dve_scan"], TILES)

            def step_c(i, c):
                s = SLOTS * i + c
                peeled = isinstance(s, int)
                slot, b = c % SLOTS, c % 2
                if not peeled or s < TILES:
                    need(pe, S["act_gt"], s - 1)
                    pe.wait_ge(x1_in[slot], 16 * (i + (c - slot) // SLOTS + 1))
                    pe.transpose(GT[b], rows[:, slot, 0, :], ident[:, :]).then_inc(S["pe_gt"], 1)
                    need(pe, S["dve_prod"], s - 1)
                    for m in range(NB):
                        last = pe.matmul(CB[b][:, cols(m, m + 1)], comp_rep[:, m, :],
                                         onehot[:, bass.ds(s * P, P)], start=True, stop=True,
                                         skip_group_check=True)
                    last.then_inc(S["pe_cb"], 1)
                if not peeled or 1 <= s <= TILES:
                    pe.wait_ge(S["dve_prod"], s)
                    need(pe, S["dve_sum"], s - 1)
                    for m in range(NB):
                        last = pe.matmul(MT, w_cen[:, W_BASE + m, :], prod[:, 1 - b, m, :],
                                         start=(m == 0), stop=(m == NB - 1))
                    last.then_inc(S["pe_mt"], 1)
                if not peeled or 2 <= s <= TILES + 1:
                    pe.wait_ge(S["dve_sum"], s - 1)
                    need(pe, S["dve_rc"], s - 2)
                    pe.transpose(ST, aggT[:, b, :], ident[:, :]).then_inc(S["pe_st"], 1)

            run_steps(pe, 0, LOOP0, LOOPS, LAST_C, step_c)

        @block.scalar
        def _(act):
            act.wait_ge(S["soft_dve"], 1)
            nc.scalar.activation(soft[:, 2:3], soft[:, 1:2], ACT.Exp, scale=-1.0).then_inc(S["soft_act"], 1)
            act.wait_ge(S["soft_act"], 1)
            nc.scalar.activation(soft[:, 3:4], soft[:, 2:3], ACT.Ln, bias=1.0).then_inc(S["soft_act"], 1)

            def root(q, lo, hi):
                return nc.scalar.activation(st[:, q, 7, lo:hi], st[:, q, 6, lo:hi], ACT.Sqrt)

            def step(i, c):
                s = SLOTS * i + c
                peeled = isinstance(s, int)
                b = c % 2
                if not peeled or s <= TILES + 1:
                    act.wait_ge(S["pe_xt"], s + 1)
                    need(act, S["pe_h"], s - 1)
                    for r in ranges(i, c):
                        last = nc.scalar.copy(xT[:, b, r[0]:r[1], :].rearrange("p c d -> p (c d)"),
                                              XT[:, cols(*r)])
                    last.then_inc(S["act_xt"], 1)
                if not peeled or 3 <= s:
                    lo, hi = span(i, c, 3)
                    act.wait_ge(S["dve_r3"], s - 2)
                    need(act, out_stored[b], 16 * halves(i, c, 3 + (1 - b)))
                    if lo == 0:
                        root(2, 0, CH).then_inc(S["act_own"], 1)
                        act.wait_ge(S["act_own"], s - 2)
                        for m in range(CH):
                            last = nc.scalar.activation(outb[:, b, m, :], Y[:, cols(m, m + 1)], ACT.Copy,
                                                        scale=st[:, 2, 7, m:m + 1])
                    if hi == CH + 1:
                        last = nc.scalar.copy(y_root[:, bass.ds((s - 4) * D, D)], Y[:, cols(DST, DST + 1)])
                    last.then_inc(S["act_out"], 1)
                if not peeled or s <= TILES + 1:
                    act.wait_ge(S["dve_q1"], s + 1)
                    root(0, 0, CH + 2).then_inc(S["act_s1"], 1)
                if not peeled or 2 <= s <= TILES + 2:
                    lo, hi = span(i, c, 2)
                    act.wait_ge(S["dve_q2"], s - 1)
                    root(1, lo, hi).then_inc(S["act_s2"], 1)
                    act.wait_ge(S["pe_vt"], s)
                    need(act, S["pe_y"], s - 3)
                    nc.scalar.copy(x1T[:, b, lo:hi, :].rearrange("p c d -> p (c d)"), VT[:, cols(lo, hi)]) \
                        .then_inc(S["act_vt"], 1)

            run_steps(act, 0, LOOP0, LOOPS, LAST_A, step)

            def step_c(i, c):
                s = SLOTS * i + c
                peeled = isinstance(s, int)
                b = c % 2
                if not peeled or s < TILES:
                    act.wait_ge(S["pe_gt"], s + 1)
                    need(act, S["dve_prod"], s - 1)
                    nc.scalar.copy(xT[:, b, 0, :], GT[b]).then_inc(S["act_gt"], 1)
                if not peeled or 3 <= s:
                    slot = c % SLOTS
                    act.wait_ge(S["dve_rc"], s - 2)
                    need(act, out_scattered[slot], 16 * scatters_before(i, c))
                    root(b, 0, 1).then_inc(S["act_own"], 1)
                    act.wait_ge(S["act_own"], GROUPS + s - 2)
                    nc.scalar.activation(rows[:, slot, 3, :], hn[:, 1 - b, 0, :], ACT.Copy,
                                         scale=st[:, b, 7, 0:1]).then_inc(S["act_oc"], 1)

            run_steps(act, 0, LOOP0, LOOPS, LAST_C, step_c)

        @block.vector
        def _(dve):
            own = Chain(dve, S["dve_own"])
            own.per_loop = 0

            own.mark(dve.memset(bn[:, :, :, :], 0.0))
            dve.wait_ge(S["weights_in"], 16 * N_W)
            dve.wait_ge(S["ident_ready"], 1)
            own.link(dve.tensor_tensor(w_raw[:, W_ROOT, :], w_raw[:, W_ROOT, :], ident[:, :], ALU.add))
            own.link(dve.tensor_reduce(row_mean[:, 0:12], w_raw[:, :, :], AX_X, ALU.add))
            own.link(dve.tensor_scalar(row_mean[:, 0:12], row_mean[:, 0:12], 1.0 / D, None, ALU.mult))
            own.mark(dve.tensor_tensor(w_cen[:, :, :], w_raw[:, :, :],
                                       row_mean[:, 0:12].unsqueeze(2).broadcast_to([P, 12, D]), ALU.subtract))
            own.link(dve.tensor_reduce(row_mean[:, 12:15], vec_raw[:, 0:3, :], AX_X, ALU.add))
            own.link(dve.tensor_scalar(row_mean[:, 12:15], row_mean[:, 12:15], 1.0 / D, None, ALU.mult))
            own.link(dve.tensor_tensor(vec_cen[:, :, :], vec_raw[:, 0:3, :],
                                       row_mean[:, 12:15].unsqueeze(2).broadcast_to([P, 3, D]), ALU.subtract))
            dve.wait_ge(S["const_ready"], 5)
            both = vec_cen[:, 0:2, :].rearrange("p v d -> p (v d)")
            own.mark(dve.tensor_scalar(part_mask[:, 0, 0:1], part_id[:, :], 0.0, None, ALU.is_equal))
            own.mark(dve.tensor_scalar(part_mask[:, 0, 1:2], part_id[:, :], 1.0, None, ALU.is_equal))
            own.mark(dve.tensor_scalar(part_mask[:, 0, 2:3], part_id[:, :], 2.0, None, ALU.is_equal))
            own.mark(dve.tensor_scalar(part_mask[:, 1, 0:1], part_id[:, :], float(REL), None, ALU.is_lt))
            own.mark(dve.tensor_scalar(part_mask[:, 1, 2:3], part_id[:, :], float(2 * REL), None, ALU.is_ge))
            own.link(dve.tensor_scalar(part_mask[:, 1, 1:2], part_id[:, :], float(REL), None, ALU.is_ge))
            own.mark(dve.tensor_tensor(part_mask[:, 1, 1:2], part_mask[:, 1, 1:2], part_mask[:, 1, 2:3],
                                       ALU.subtract))

            def split3(value, parts, rem):
                own.link(dve.tensor_copy(parts[0], value))
                own.link(dve.tensor_tensor(rem[0], value, parts[0], ALU.subtract))
                own.link(dve.tensor_copy(parts[1], rem[0]))
                own.link(dve.tensor_tensor(rem[1], rem[0], parts[1], ALU.subtract))
                own.link(dve.tensor_copy(parts[2], rem[1]))

            split3(both[0:PARTS], [split[0:PARTS, k, :] for k in range(PARTS)],
                   [rest[0:PARTS, k, :] for k in range(2)])
            own.link(dve.tensor_scalar(rest[0:PARTS, 0, :], split[0:PARTS, 0, :], part_mask[0:PARTS, 0, 0:1], None,
                                       ALU.mult))
            for k in range(1, PARTS):
                own.link(dve.scalar_tensor_tensor(rest[0:PARTS, 0, :], split[0:PARTS, k, :],
                                                  part_mask[0:PARTS, 0, k:k + 1], rest[0:PARTS, 0, :],
                                                  ALU.mult, ALU.add))
            for v in range(2):
                own.mark(dve.tensor_copy(bias3[:, v, :].rearrange("p (c d) -> p c d", c=CH),
                                         rest[0:PARTS, 0:1, cols(v, v + 1)].broadcast_to([PARTS, CH, D])))
            K3 = PARTS * REL
            split3(comp_raw[:, :], [comp_split[:, k, :] for k in range(PARTS)],
                   [comp_rest[:, k, :] for k in range(2)])
            own.link(dve.tensor_scalar(comp_rest[:, 0, :], comp_split[:, 0, :], part_mask[0:K3, 1, 0:1], None,
                                       ALU.mult))
            for k in range(1, PARTS):
                own.link(dve.scalar_tensor_tensor(comp_rest[:, 0, :], comp_split[:, k, :],
                                                  part_mask[0:K3, 1, k:k + 1], comp_rest[:, 0, :],
                                                  ALU.mult, ALU.add))
            own.mark(dve.tensor_copy(comp_rep[:, :, :],
                                     comp_rest[:, 0, :].unsqueeze(2).broadcast_to([K3, NB, P])))
            own.link(dve.tensor_scalar(soft[:, 4:5], soft[:, 0:1], -1.0, None, ALU.mult))
            dve.tensor_tensor(soft[:, 1:2], soft[:, 0:1], soft[:, 4:5], ALU.max).then_inc(S["soft_dve"], 1)
            dve.wait_ge(S["soft_act"], 2)
            own.link(dve.tensor_scalar(soft[:, 5:6], soft[:, 0:1], 0.0, soft[:, 3:4], ALU.max, ALU.add))
            dve.wait_ge(S["edges_in"], 16 * N_EDGE)
            own.mark(dve.tensor_scalar(e_scale[:, :], e_weight[:, :], soft[:, 5:6], 1.0, ALU.mult, ALU.add))
            own.link(dve.tensor_tensor(same_next[:, :], dst_i[:, :], dst_n[:, :], ALU.is_equal))
            dve.scalar_tensor_tensor(scat_i[:, :], same_next[:, :], float(SKIP), dst_i[:, :],
                                     ALU.mult, ALU.add).then_inc(S["scat_ready"], 1)
            own.link(dve.tensor_scalar(rel_id[:, :], part_mask[0:K3, 1, 1:2], -float(REL), part_id[0:K3, :],
                                       ALU.mult, ALU.add))
            own.link(dve.scalar_tensor_tensor(rel_id[:, :], part_mask[0:K3, 1, 2:3], -float(2 * REL), rel_id[:, :],
                                              ALU.mult, ALU.add))
            dve.wait_ge(S["types_in"], 16)
            own.link(dve.tensor_scalar(onehot[:, :], types[0:K3, :], rel_id[:, 0:1], None, ALU.is_equal))
            dve.wait_ge(S["line_in"], 16)
            own.link(dve.tensor_tensor(same_prev[:, :], line[:, 1:EP + 1], line[:, 0:EP], ALU.is_equal))
            dve.tensor_tensor_scan(pos[0:1, :], same_prev[0:1, :], same_prev[0:1, :], 0.0, ALU.mult,
                                   ALU.add).then_inc(S["pos_ready"], 1)
            dve.wait_ge(S["pos_cols"], 1)
            own.link(dve.tensor_scalar(inv_deg[:, :], H[:, 0:TILES], 1.0, None, ALU.add))
            dve.reciprocal(inv_deg[:, :], inv_deg[:, :]).then_inc(S["setup_dve"], 1)

            def inverse_variance(q, lo, hi):
                me, m2e, mo, m2o = (bn[:, q, lo:hi, k] for k in (1, 2, 4, 5))
                d, m2, var, inv = (st[:, q, k, lo:hi] for k in (0, 1, 2, 6))
                own.mark(dve.tensor_tensor(d, me, mo, ALU.subtract))
                own.link(dve.tensor_tensor(m2, m2e, m2o, ALU.add))
                own.mark(dve.scalar_tensor_tensor(var, d, 0.25, d, ALU.mult, ALU.mult))
                own.link(dve.tensor_scalar(m2, m2, 1.0 / D, LN_EPS, ALU.mult, ALU.add))
                own.link(dve.tensor_tensor(var, var, m2, ALU.add))
                return dve.reciprocal(inv, var)

            def y_stats(i, c):
                s = SLOTS * i + c
                lo, hi = span(i, c, 3)
                dve.wait_ge(S["pe_y"], s - 2)
                if lo < CH:
                    for m in range(CH):
                        own.mark(dve.bn_stats(bn[:, 2, m, :], Y[:, cols(m, m + 1)]))
                    own.need(own.count)
                    inverse_variance(2, 0, CH).then_inc(S["dve_r3"], 1)
                else:
                    dve.bn_stats(bn[:, 2, DST, :], Y[:, cols(DST, DST + 1)]).then_inc(S["dve_r3"], 1)

            def step(i, c):
                s = SLOTS * i + c
                peeled = isinstance(s, int)
                slot, b = c % SLOTS, c % 2
                if not peeled or 3 <= s:
                    y_stats(i, c)
                if not peeled or s <= TILES + 1:
                    lo, hi = span(i, c, 1)
                    src = not peeled or s < TILES
                    dve.wait_ge(S["pe_h"], s + 1)
                    if src:
                        hp_at = own.mark(dve.scalar_tensor_tensor(hp[:, :], H[:, cols(SRC, SRC + 1)],
                                                          e_scale[:, bass.ds(s, 1)], vec_cen[:, 2, :],
                                                          ALU.mult, ALU.add))
                    for m in range(lo, hi):
                        own.mark(dve.bn_stats(bn[:, 0, m, :], H[:, cols(m, m + 1)]))
                    if src:
                        own.need(hp_at)
                        own.mark(dve.bn_stats(bn[:, 0, SRC, :], hp[:, :]))
                    own.need(own.count)
                    inverse_variance(0, 0, CH + 2).then_inc(S["dve_q1"], 1)

                if not peeled or 2 <= s <= TILES + 2:
                    lo, hi = span(i, c, 2)
                    pb = 1 - b
                    dve.wait_ge(S["pool_b"], s - 1)
                    h = hn[:, pb, lo:hi, :].rearrange("p c d -> p (c d)")
                    own.link(dve.scalar_tensor_tensor(
                        h, h, 0.0, rows[:, (c - 1) % SLOTS, lo:hi, :].rearrange("p c d -> p (c d)"),
                        ALU.max, ALU.add))
                    for m in range(lo, hi):
                        own.mark(dve.bn_stats(bn[:, 1, m, :], hn[:, pb, m, :]))
                    own.need(own.count)
                    own.link(dve.tensor_tensor(st[:, 1, 3, lo:hi], bn[:, 1, lo:hi, 1], bn[:, 1, lo:hi, 4], ALU.add))
                    own.mark(dve.tensor_scalar(st[:, 1, 4, lo:hi], st[:, 1, 3, lo:hi], 0.5, None, ALU.mult))
                    inverse_variance(1, lo, hi).then_inc(S["dve_q2"], 1)

                if not peeled or s <= TILES + 1:
                    lo, hi = span(i, c, 1)
                    dve.wait_ge(S["act_s1"], s + 1)
                    if src:
                        need(dve, S["pe_vt"], s - 1)
                        last = dve.scalar_tensor_tensor(pooled[:, b, :], hp[:, :], st[:, 0, 7, SRC:SRC + 1],
                                                        vec_raw[:, GAM_P, :], ALU.mult, ALU.mult)
                        if lo < hi:
                            own.mark(last)
                    for m in range(lo, hi):
                        last = dve.scalar_tensor_tensor(hn[:, b, m, :], H[:, cols(m, m + 1)],
                                                        st[:, 0, 7, m:m + 1], vec_raw[:, GAM_F, :],
                                                        ALU.mult, ALU.mult)
                        if m < hi - 1:
                            own.mark(last)
                    last.then_inc(S["dve_t"], 1)
                if not peeled or 2 <= s <= TILES + 2:
                    lo, hi = span(i, c, 2)
                    dve.wait_ge(S["act_s2"], s - 1)
                    if not peeled or s >= 4:
                        need(dve, S["pe_vt"], s - 2)
                        need(dve, S["pool_xd"], s - 4)
                        n = halves(i, c, 2 + b)
                        need(dve, x1_stored[b], 16 * n)
                    for m in range(lo, hi):
                        last = dve.tensor_scalar(x1[:, b, m, :], hn[:, pb, m, :], st[:, 1, 4, m:m + 1],
                                                 st[:, 1, 7, m:m + 1], ALU.subtract, ALU.mult)
                        if m < hi - 1:
                            own.mark(last)
                    last.then_inc(S["dve_x1"], 1)
                if not peeled or 1 <= s <= TILES:
                    dve.wait_ge(S["pe_vt"], s)
                    need(dve, S["act_vt"], s - 1)
                    need(dve, S["pe_h"], s)
                    need(dve, S["dve_scan"], s - 1)
                    first = 0.0 if peeled and s == 1 else aggT[:, b, D - 1:D]
                    dve.tensor_tensor_scan(aggT[:, 1 - b, :], same_prev[:, bass.ds((s - 1) * P, P)],
                                           VT[:, cols(SRC, SRC + 1)], first, ALU.mult, ALU.max) \
                       .then_inc(S["dve_scan"], 1)

            own.per_loop = SLOTS * (9 + 17 + 17)
            run_steps(dve, 0, LOOP0, LOOPS, LAST_A, step, own)

            dve.wait_ge(S["pool_xd"], TILES)

            def move(i, c):
                t = SLOTS * i + c
                slot = c % SLOTS
                need(dve, x1_scattered[slot], 16 * (i + (c - slot) // SLOTS))
                dve.tensor_copy(rows[:, slot, 0, :], x1_dst[:, bass.ds(t, 1), :].rearrange("p t d -> p (t d)")) \
                   .then_inc(S["dve_move"], 1)

            run_steps(dve, 0, LOOP0, LOOPS, TILES - 1, move)

            own = Chain(dve, S["c_own"])
            own.per_loop = SLOTS * 7

            def step_c(i, c):
                s = SLOTS * i + c
                peeled = isinstance(s, int)
                b = c % 2
                if not peeled or s < TILES:
                    dve.wait_ge(S["act_gt"], s + 1)
                    dve.wait_ge(S["pe_cb"], s + 1)
                    need(dve, S["pe_mt"], s - 1)
                    dve.tensor_tensor(prod[:, b, :, :], CB[b].rearrange("p (b d) -> p b d", b=NB),
                                      xT[:, b, 0:1, :].broadcast_to([P, NB, D]), ALU.mult) \
                       .then_inc(S["dve_prod"], 1)
                if not peeled or 1 <= s <= TILES:
                    dve.wait_ge(S["pe_mt"], s)
                    need(dve, S["pe_st"], s - 2)
                    need(dve, S["dve_sum"], s - 1)
                    first = 0.0 if peeled and s == 1 else aggT[:, b, D - 1:D]
                    dve.tensor_tensor_scan(aggT[:, 1 - b, :], same_prev[:, bass.ds((s - 1) * P, P)], MT,
                                           first, ALU.mult, ALU.add).then_inc(S["dve_sum"], 1)
                if not peeled or 2 <= s <= TILES + 1:
                    t = s - 2
                    dve.wait_ge(S["pe_st"], s - 1)
                    need(dve, S["act_oc"], s - 3)
                    own.link(dve.scalar_tensor_tensor(hn[:, b, 0, :], ST, inv_deg[:, bass.ds(t, 1)],
                                                      y_root[:, bass.ds(t * D, D)], ALU.mult, ALU.add))
                    own.link(dve.bn_stats(bn[:, 1 - b, 0, :], hn[:, b, 0, :]))
                    inverse_variance(1 - b, 0, 1).then_inc(S["dve_rc"], 1)

            run_steps(dve, 0, LOOP0, LOOPS, LAST_C, step_c, own)


def kernel(x, src, dst, edge_type_16, edge_weight, L0_gnn_pool_w, L0_gnn_pool_b, L0_gnn_ln_pool_g,
           L0_gnn_ln_pool_b, L0_gnn_final_w, L0_gnn_final_b, L0_gnn_ln_final_g, L0_gnn_ln_final_b,
           L0_gnn_coeff_raw, L1_gnn_weight, L1_gnn_comp, L1_gnn_bias):
    import numpy as np
    import concourse.bacc as bacc
    from concourse.bass_utils import run_bass_kernel_spmd

    x, src, dst, edge_type, edge_weight = (np.asarray(a) for a in (x, src, dst, edge_type_16, edge_weight))
    N, E = x.shape[0], src.shape[0]
    tiles = -(-E // P)

    def line(a, fill, extra=0):
        return np.concatenate([a, np.full(tiles * P + extra - E, fill, a.dtype)])

    def by_tile(a):
        return np.ascontiguousarray(a.reshape(tiles, P).T)

    dst_ext = line(dst, N, 1)
    arrays = {
        "x": x,
        "src_cols": by_tile(line(src, 0)),
        "dst_cols": by_tile(dst_ext[:-1]),
        "dst_next_cols": by_tile(dst_ext[1:]),
        "dst_line": np.concatenate([np.full(1, -1, dst.dtype), dst_ext[:-1]])[None, :],
        "type_line": line(edge_type, 0)[None, :],
        "weight_cols": by_tile(line(edge_weight, 0)),
        "pool_w": L0_gnn_pool_w, "pool_b": L0_gnn_pool_b, "ln_pool_g": L0_gnn_ln_pool_g,
        "ln_pool_b": L0_gnn_ln_pool_b, "final_w": L0_gnn_final_w, "final_b": L0_gnn_final_b,
        "ln_final_g": L0_gnn_ln_final_g, "ln_final_b": L0_gnn_ln_final_b, "coeff_raw": L0_gnn_coeff_raw,
        "weight": L1_gnn_weight, "comp": L1_gnn_comp, "bias": L1_gnn_bias,
    }
    nc = bacc.Bacc("TRN2", target_bir_lowering=False, num_devices=1)
    feed, aps = {}, {}
    for name, a in arrays.items():
        a = np.asarray(a)
        a = np.ascontiguousarray(a.reshape(1, -1) if a.ndim < 2 else a)
        feed[f"in_{name}"] = a
        aps[name] = nc.dram_tensor(f"in_{name}", a.shape, mybir.dt.from_np(a.dtype), kind="ExternalInput").ap()
    aps["out"] = nc.dram_tensor("out_rows", x.shape, F32, kind="ExternalOutput").ap()
    gnn_kernel(nc, **aps)
    r = run_bass_kernel_spmd(nc, [feed], core_ids=[0])
    return r.results[0]["out_rows"]
```

```python
from contextlib import ExitStack

import concourse.bass as bass
from concourse import mybir

P = 128
CH = 4
SRC = CH
NB = 8
REL = 16
PARTS = 3
LN_EPS = 1e-5
SKIP = 1 << 20
SLOTS = 4
PAIR = 2

ALU = mybir.AluOpType
ACT = mybir.ActivationFunctionType
F32 = mybir.dt.float32
BF16 = mybir.dt.bfloat16
I32 = mybir.dt.int32
U32 = mybir.dt.uint32
U8 = mybir.dt.uint8
AX_X = mybir.AxisListType.X


def need(eng, sem, count):
    if isinstance(count, int) and count <= 0:
        return
    eng.wait_ge(sem, count)


class Chain:

    def __init__(self, eng, sem):
        self.eng, self.sem, self.count, self.base = eng, sem, 0, 0

    def mark(self, ins):
        ins.then_inc(self.sem, 1)
        self.count += 1
        return self.count

    def need(self, at):
        self.eng.wait_ge(self.sem, self.base + at)

    def link(self, ins):
        self.need(self.mark(ins))


def run_steps(eng, plan, step, chain=None, marks=()):
    marks = list(marks)
    for first, last, looped in plan:
        if not looped:
            for s in range(first, last + 1):
                step(0, s)
            continue
        assert first % SLOTS == 0 and (last - first + 1) % SLOTS == 0
        loops = (last - first + 1) // SLOTS
        with eng.Fori(0, loops) as i:
            if chain:
                before, base, per_pass = chain.count, chain.base, marks.pop(0)
                chain.base = i * per_pass + base
            for c in range(first, first + SLOTS):
                step(i, c)
        if chain:
            assert chain.count - before == per_pass, ("marks in a pass", chain.count - before)
            chain.base = base + (loops - 1) * per_pass


def gnn_kernel(nc, x, src_cols, dst_cols, dst_next_cols, dst_line, dst_rows, dst_prev_rows, type_line,
               weight_cols, pool_w, pool_b, ln_pool_g, ln_pool_b, final_w, final_b, ln_final_g, ln_final_b,
               coeff_raw, weight, comp, bias, out):
    N, D = x.shape
    TILES = src_cols.shape[1]
    EP = TILES * P
    ROWS = CH * P
    DENSE = -(-N // ROWS)
    TAIL = (N - (DENSE - 1) * ROWS) // CH
    EDGE = -(-TILES // CH)
    GROUPS = DENSE + EDGE
    LAST_TILES = TILES - (EDGE - 1) * CH
    PAIRS = TILES // PAIR
    assert DENSE == TILES and D == P and (N - (DENSE - 1) * ROWS) % CH == 0 and TILES % PAIR == 0

    LAST_A = GROUPS + 6
    LOOP_A = 2 * SLOTS
    LOOP_A_END = LOOP_A + (DENSE - 2 - LOOP_A) // SLOTS * SLOTS
    LOOP_E = -(-(DENSE + 7) // SLOTS) * SLOTS
    LOOP_E_END = LOOP_E + (GROUPS - 1 - LOOP_E) // SLOTS * SLOTS
    PLAN_A = [(0, LOOP_A - 1, False), (LOOP_A, LOOP_A_END - 1, True), (LOOP_A_END, LOOP_E - 1, False),
              (LOOP_E, LOOP_E_END - 1, True), (LOOP_E_END, LAST_A, False)]
    LAST_C = PAIRS + 3
    LOOP_C = 2 * SLOTS
    LOOP_C_END = LOOP_C + (PAIRS - 2 - LOOP_C) // SLOTS * SLOTS
    PLAN_C = [(0, LOOP_C - 1, False), (LOOP_C, LOOP_C_END - 1, True), (LOOP_C_END, LAST_C, False)]

    x1_table = nc.dram_tensor("x1_table", [N, D], F32).ap()
    x_dst_table = nc.dram_tensor("x_dst_table", [P, TILES * D], F32).ap()

    with ExitStack() as ctx:
        def sb(name, shape, dt=F32):
            return ctx.enter_context(nc.sbuf_tensor(name, shape, dt))

        def sem(name):
            return ctx.enter_context(nc.semaphore(name))

        ident = sb("ident", [P, P])
        part_id = sb("part_id", [P, 1])
        row_mean = sb("row_mean", [P, 16])
        w_cen = sb("w_cen", [P, 12, D])
        vec_raw = sb("vec_raw", [P, 7, D])
        vec_cen = sb("vec_cen", [P, 3, D])
        split = sb("split", [PARTS, PARTS, 2 * D], BF16)
        rest = sb("rest", [PARTS, 2, 2 * D])
        bias3 = sb("bias3", [PARTS, 2, CH * D], BF16)
        ones3 = sb("ones3", [PARTS, P], BF16)
        comp_raw = sb("comp_raw", [PARTS * REL, NB])
        comp_split = sb("comp_split", [PARTS * REL, PARTS, NB], BF16)
        comp_rest = sb("comp_rest", [PARTS * REL, 2, NB])
        comp_rep = sb("comp_rep", [PARTS * REL, NB, P], BF16)
        part_mask = sb("part_mask", [P, 2, PARTS])
        rel_id = sb("rel_id", [PARTS * REL, 1])
        one = sb("one", [P, 1])
        soft = sb("soft", [P, 6])
        src_i = sb("src_i", [P, TILES], I32)
        dst_i = sb("dst_i", [P, TILES], I32)
        dst_n = sb("dst_n", [P, TILES], I32)
        scat_i = sb("scat_i", [P, TILES], I32)
        idx = sb("idx", [P, SLOTS, CH], I32)
        same_next = sb("same_next", [P, TILES])
        e_scale = sb("e_scale", [P, TILES])
        e_weight = sb("e_weight", [P, TILES])
        inv_deg = sb("inv_deg", [P, TILES])
        same_prev = sb("same_prev", [P, EP], U8)
        onehot = sb("onehot", [PARTS * REL, EP], BF16)
        d_cur = sb("d_cur", [TILES, P], I32)
        d_prev = sb("d_prev", [TILES, P], I32)
        carry = sb("carry", [1, 3, P])
        carry_col = sb("carry_col", [TILES, 1])
        rows = sb("rows", [P, SLOTS, CH + 1, D])
        x_dst = sb("x_dst", [P, SLOTS, D])
        xT = sb("xT", [P, 2, CH + 1, D])
        hp = sb("hp", [P, D])
        pooled = sb("pooled", [P, 2, D])
        work = sb("work", [P, 8 * CH, D])
        agg_now = sb("agg_now", [P, 2, CH, D])
        outb = sb("outb", [P, 2, CH, D])
        junk = sb("junk", [P, 2, CH, D], BF16)
        bn = sb("bn", [P, 2 * CH + 1, 6])
        st = sb("st", [P, 8, 3 * CH + 1])
        ysq = sb("ysq", [P, 2, CH])
        agg_all = sb("agg_all", [P, EDGE * CH, D])
        y_root = sb("y_root", [P, EDGE * CH * D + 1])

        w_raw = agg_all[:, 0:12, :]
        zero = hp
        x1 = work[:, 0:2 * CH, :].rearrange("p (b c) d -> p b c d", b=2)
        x1T = work[:, 2 * CH:4 * CH, :].rearrange("p (b c) d -> p b c d", b=2)
        hn = work[:, 4 * CH:8 * CH, :].rearrange("p (b c) d -> p b c d", b=4)
        agg_line = agg_all[:, :, :].rearrange("p t d -> p (t d)")
        line = y_root[:, :].bitcast(I32)
        types = agg_line.bitcast(I32)
        seg = agg_now[0:TILES, :, :, :].rearrange("p b c d -> p (b c) d")
        prod = work[:, :, :].rearrange("p (b m t) d -> p b m t d", b=2, m=NB)
        sums = agg_now[:, 0, :, :].rearrange("p (b t) d -> p b t d", b=2)
        y_rows = agg_now[:, 1, :, :].rearrange("p (b t) d -> p b t d", b=2)

        ps = ctx.enter_context(nc.psum_tensor("ps", [P, 8, 512], F32))

        def banks(a, n):
            return ps[:, a:a + n, :].rearrange("p b n -> p (b n)")

        XT, H = banks(0, 2), [banks(2, 1), banks(3, 1)]
        VT, HE, PT = banks(4, 1), ps[:, 5, 0:D], ps[:, 5, D:2 * D]
        Y = [banks(6, 1), banks(7, 1)]
        CB = [banks(0, 2), banks(2, 2)]
        GT, MT, ST = banks(4, 1), [banks(5, 1), banks(6, 1)], banks(7, 1)

        names = ("weights_in", "edges_in", "line_in", "line_rest_in", "types_in", "const_ready", "ident_ready", "scat_ready",
                 "setup_dve", "soft_dve", "soft_act", "pe_a", "act_a", "pe_b", "pe_e", "dve_q", "act_q", "dve_m",
                 "dve_t", "dve_te", "pool_b", "pool_p", "dve_v", "act_x", "pe_c", "pe_cp", "act_c", "dve_scan", "pe_d",
                 "act_y", "act_o", "dve_own", "idx_ready", "deg_dve", "deg_pe", "c_own", "pe_g", "act_g",
                 "pe_cb", "dve_prod", "pe_m", "dve_sum", "pe_s", "dve_r", "act_r", "act_out")
        S = {n: sem(n) for n in names}

        def sems(name, n):
            return [sem(f"{name}{j}") for j in range(n)]

        rows_in, dst_in, src_in = sems("rows_in", SLOTS), sems("dst_in", SLOTS), sems("src_in", SLOTS)
        dst_stored = sems("dst_stored", SLOTS)
        x1_stored, x1_scattered, out_stored = sems("x1_stored", 2), sems("x1_scattered", 2), sems("out_stored", 2)
        x1_in, out_scattered = sems("x1_in", SLOTS), sems("out_scattered", SLOTS)

        full = (DENSE - 1) * ROWS
        x_groups, x1_groups, out_groups = (
            t[0:full, :].rearrange("(g p c) d -> g p (c d)", p=P, c=CH) for t in (x, x1_table, out))
        x_tail, x1_tail, out_tail = (t[full:N, :].rearrange("(p c) d -> p (c d)", c=CH) for t in (x, x1_table, out))

        W_TOP, W_BOT, W_POOL, W_BASE, W_ROOT = 0, 1, 2, 3, 11
        GAM_F, BET_F, GAM_P, BET_P = 3, 4, 5, 6
        N_W, N_EDGE, N_CONST = 7 + 4 + 1 + PARTS, 6, 8
        FIRST_LINE = 16 * P
        RES, ROOT = CH + 1, 2 * CH + 1

        def cols(a, b):
            return slice(a * D, b * D)

        def is_group(c, k):
            return 0 <= c - k < GROUPS

        def is_dense(c, k):
            return 0 <= c - k < DENSE

        def is_tile(c, k):
            return 0 <= c - k < TILES

        def since(i, c, first, every):
            assert (c - first) % every == 0
            return SLOTS // every * i + (c - first) // every

        block = ctx.enter_context(nc.Block())

        @block.sync
        def _(sp):
            def load(i, c):
                g, slot = SLOTS * i + c, c % SLOTS
                flat = rows[:, slot, 0:CH, :].rearrange("p c d -> p (c d)")
                if c == DENSE - 1:
                    into, of = flat[0:TAIL], x_tail
                elif c < DENSE:
                    into, of = flat, x_groups[g]
                elif c == GROUPS - 1:
                    into, of = flat[:, 0:LAST_TILES * D], x_dst_table[:, (g - DENSE) * CH * D:TILES * D]
                else:
                    into, of = flat, x_dst_table[:, bass.ds((g - DENSE) * CH * D, CH * D)]
                sp.dma_start(into, of).then_inc(rows_in[slot], 16)

            for w, ap in ((W_TOP, final_w[0:D, :]), (W_BOT, final_w[D:2 * D, :]), (W_POOL, pool_w)):
                sp.dma_start(w_raw[:, w, :], ap).then_inc(S["weights_in"], 16)
            sp.dma_start(w_raw[:, W_BASE:W_ROOT + 1, :], weight.rearrange("b k n -> k b n")) \
                .then_inc(S["weights_in"], 16)
            for v, ap in enumerate((final_b, bias, pool_b, ln_final_g, ln_final_b, ln_pool_g, ln_pool_b)):
                sp.dma_start(vec_raw[:, v, :], ap.broadcast_to([P, D])).then_inc(S["weights_in"], 16)
            sp.wait_ge(S["const_ready"], N_CONST)
            load(0, 0)
            sp.dma_start(line[:, 0:FIRST_LINE + 1], dst_line[:, 0:FIRST_LINE + 1].broadcast_to([P, FIRST_LINE + 1])) \
                .then_inc(S["line_in"], 16)

            def step(i, c):
                s = SLOTS * i + c
                b = c % 2
                if is_tile(c, 0):
                    slot = c % SLOTS
                    sp.wait_ge(dst_in[slot], 16 * since(i, c + SLOTS, slot, SLOTS))
                    sp.dma_start(x_dst_table[:, bass.ds(s * D, D)], x_dst[:, slot, :]).then_inc(dst_stored[slot], 16)
                if c + 1 == DENSE:
                    for j in range(SLOTS):
                        sp.wait_ge(dst_stored[j], 16 * len(range(j, TILES, SLOTS)))
                if is_group(c, -1):
                    need(sp, S["dve_v"], s - 2)
                    load(i, c + 1)
                if c == 2:
                    sp.dma_start(line[:, FIRST_LINE + 1:EP + 1],
                                 dst_line[:, FIRST_LINE + 1:EP + 1].broadcast_to([P, EP - FIRST_LINE])) \
                        .then_inc(S["line_rest_in"], 16)
                if is_dense(c, 4):
                    sp.wait_ge(S["act_x"], s - 3)
                    b_ = x1[:, b, :, :].rearrange("p c d -> p (c d)")
                    tail = c - 4 == DENSE - 1
                    sp.dma_start(x1_tail if tail else x1_groups[s - 4], b_[0:TAIL] if tail else b_) \
                        .then_inc(x1_stored[b], 16)
                if is_dense(c, 7):
                    sp.wait_ge(S["act_o"], s - 6)
                    b_ = outb[:, b, :, :].rearrange("p c d -> p (c d)")
                    tail = c - 7 == DENSE - 1
                    sp.dma_start(out_tail if tail else out_groups[s - 7], b_[0:TAIL] if tail else b_) \
                        .then_inc(out_stored[b], 16)

            run_steps(sp, PLAN_A, step)
            sp.wait_ge(S["act_a"], GROUPS)
            sp.dma_start(types[0:PARTS * REL, 0:EP], type_line.broadcast_to([PARTS * REL, EP])) \
                .then_inc(S["types_in"], 16)

        @block.gpsimd
        def _(pool):
            pool.memset(zero[:, :], 0.0).then_inc(S["const_ready"], 1)
            pool.memset(one[:, :], 1.0).then_inc(S["const_ready"], 1)
            pool.memset(ones3[:, :], 1.0).then_inc(S["const_ready"], 1)
            pool.iota(part_id[:, :], [[0, 1]], base=0, channel_multiplier=1,
                      allow_small_or_imprecise_dtypes=True).then_inc(S["const_ready"], 1)
            pool.memset(rows[:, :, :, :], 0.0).then_inc(S["const_ready"], 1)
            pool.memset(x_dst[:, :, :], 0.0).then_inc(S["const_ready"], 1)
            pool.memset(agg_all[:, TILES:EDGE * CH, :], 0.0).then_inc(S["const_ready"], 1)
            pool.memset(carry[:, :, :], 0.0).then_inc(S["const_ready"], 1)
            pool.wait_ge(S["const_ready"], N_CONST)
            pool.affine_select(out=ident[:, :], in_=zero[:, :], compare_op=ALU.not_equal, fill=1.0, base=0,
                               pattern=[[-1, P]], channel_multiplier=1).then_inc(S["ident_ready"], 1)
            pool.wait_ge(S["edges_in"], 16 * N_EDGE)
            last_node = pool.to_reg(N - 1)

            def fetch(*pairs):
                for to, of in pairs:
                    pool.tensor_copy(to, of).then_inc(S["idx_ready"], 1)

            def indirect(*args):
                pool.nop(nofuse=True)
                return pool.indirect_dma_start(*args, bounds_check=last_node, oob_is_err=False)

            def by(slot, n):
                return bass.IndirectOffsetOnAxis(ap=idx[:, slot, n:n + 1].bitcast(U32), axis=0)

            def gather(i, c):
                t, slot = SLOTS * i + c, c % SLOTS
                fetch((idx[:, slot, 0:1], src_i[:, bass.ds(t, 1)]), (idx[:, slot, 1:2], dst_i[:, bass.ds(t, 1)]))
                pool.wait_ge(S["idx_ready"], 2 * t + 2)
                indirect(rows[:, slot, SRC, :], None, x[:, :], by(slot, 0)).then_inc(src_in[slot], 16)
                indirect(x_dst[:, slot, :], None, x[:, :], by(slot, 1)).then_inc(dst_in[slot], 16)

            gather(0, 0)
            gather(0, 1)

            def step(i, c):
                s = SLOTS * i + c
                b = c % 2
                if is_group(c, 1):
                    if is_tile(c, 1):
                        pool.wait_ge(S["dve_te"], s)
                        q = pooled[:, b, :]
                        pool.tensor_tensor(q, q, vec_raw[:, BET_P, :], ALU.add).then_inc(S["pool_p"], 1)
                    pool.wait_ge(S["dve_t"], s)
                    h = hn[:, (c - 1) % SLOTS, :, :]
                    pool.tensor_tensor(h, h, vec_raw[:, BET_F:BET_F + 1, :].broadcast_to([P, CH, D]),
                                       ALU.add).then_inc(S["pool_b"], 1)
                if is_tile(c, -2):
                    slot = (c + 2) % SLOTS
                    need(pool, S["pe_a"], s - 1)
                    if c + 2 >= SLOTS:
                        pool.wait_ge(dst_stored[slot], 16 * since(i, c + 2, slot, SLOTS))
                    gather(i, c + 2)
                if is_group(c, 4) and not is_dense(c, 4):
                    n = LAST_TILES if c - 4 == GROUPS - 1 else CH
                    if c - 4 == DENSE:
                        for j in range(2):
                            pool.wait_ge(x1_stored[j], 16 * (DENSE // 2))
                    slot, d = c % SLOTS, s - 4 - DENSE
                    fetch((idx[:, slot, 0:n], scat_i[:, bass.ds(d * CH, n)]))
                    pool.wait_ge(S["idx_ready"], 2 * TILES + d + 1)
                    pool.wait_ge(S["act_x"], s - 3)
                    for m in range(n):
                        indirect(x1_table[:, :], by(slot, m), x1[:, b, m, :], None).then_inc(x1_scattered[b], 16)

            pool.wait_ge(S["scat_ready"], 1)
            run_steps(pool, PLAN_A, step)

            n_even = len([g for g in range(EDGE) if (g + DENSE + 4) % 2 == 0])
            for b, n in ((0, n_even), (1, EDGE - n_even)):
                short = (GROUPS + 3) % 2 == b
                pool.wait_ge(x1_scattered[b], 16 * (n * CH - (CH - LAST_TILES) * short))
            for j in range(2):
                pool.wait_ge(out_stored[j], 16 * (DENSE // 2))
            FETCHED = 2 * TILES + EDGE

            def gather_x1(i, c):
                q, slot = SLOTS * i + c, c % SLOTS
                for n in range(PAIR):
                    indirect(rows[:, slot, n, :], None, x1_table[:, :], by(slot, n)).then_inc(x1_in[slot], 16)

            def fetch_pair(i, c):
                fetch((idx[:, c % SLOTS, 0:PAIR], src_i[:, bass.ds((SLOTS * i + c) * PAIR, PAIR)]))

            for c in range(2):
                fetch_pair(0, c)
                pool.wait_ge(S["idx_ready"], FETCHED + c + 1)
                gather_x1(0, c)

            def step_c(i, c):
                s = SLOTS * i + c
                slot = c % SLOTS
                in_, out_ = c + 2 < PAIRS, 0 <= c - 4 < PAIRS
                fetched = 2 + s + (s - 4 if c >= 4 else 0) if c + 2 <= PAIRS else PAIRS + s - 4
                new = 0
                if in_:
                    need(pool, S["pe_g"], s - 1)
                    fetch_pair(i, c + 2)
                    new += 1
                if out_:
                    pool.wait_ge(S["act_out"], s - 3)
                    fetch((idx[:, slot, PAIR:2 * PAIR], scat_i[:, bass.ds((s - 4) * PAIR, PAIR)]))
                    new += 1
                pool.wait_ge(S["idx_ready"], FETCHED + fetched + new)
                if in_:
                    gather_x1(i, c + 2)
                if out_:
                    for n in range(PAIR):
                        indirect(out[:, :], by(slot, PAIR + n), outb[:, c % 2, PAIR * (c // 2 % 2) + n, :], None) \
                            .then_inc(out_scattered[slot], 16)

            run_steps(pool, PLAN_C, step_c)
            for j in range(SLOTS):
                pool.wait_ge(out_scattered[j], 16 * PAIR * len(range(j, PAIRS, SLOTS)))

        @block.tensor
        def _(pe):
            pe.wait_ge(S["ident_ready"], 1)
            pe.wait_ge(S["const_ready"], N_CONST)
            pe.wait_ge(S["setup_dve"], 1)

            def step(i, c):
                s = SLOTS * i + c
                slot, b = c % SLOTS, c % 2
                if is_group(c, 1):
                    pe.wait_ge(S["act_a"], s)
                    need(pe, S["dve_t"], s - 2)
                    edge = not is_dense(c, 1)
                    pe.matmul(H[1 - b], ones3[:, :], bias3[:, 0, :], start=True, stop=False,
                              skip_group_check=True)
                    for m in range(CH):
                        last = pe.matmul(H[1 - b][:, cols(m, m + 1)], xT[:, 1 - b, m, :], w_cen[:, W_TOP, :],
                                         start=False, stop=not edge, skip_group_check=True)
                        if edge:
                            last = pe.matmul(H[1 - b][:, cols(m, m + 1)], agg_now[:, 1 - b, m, :],
                                             w_cen[:, W_BOT, :], start=False, stop=True, skip_group_check=True)
                    last.then_inc(S["pe_b"], 1)
                if is_tile(c, 2):
                    pe.wait_ge(S["pool_p"], s - 1)
                    need(pe, S["dve_scan"], s - 2)
                    pe.transpose(PT, pooled[:, 1 - b, :], ident[:, :]).then_inc(S["pe_cp"], 1)
                if is_tile(c, 1):
                    pe.matmul(HE, xT[:, 1 - b, SRC, :], w_cen[:, W_POOL, :],
                              start=True, stop=True).then_inc(S["pe_e"], 1)
                if is_group(c, 5):
                    pe.wait_ge(S["act_x"], s - 4)
                    need(pe, S["act_c"], s - 5)
                    for m in range(CH):
                        last = pe.transpose(VT[:, cols(m, m + 1)], x1[:, 1 - b, m, :], ident[:, :])
                    last.then_inc(S["pe_c"], 1)
                if is_group(c, 0):
                    need(pe, S["act_a"], s)
                    pe.wait_ge(rows_in[slot], 16 * since(i, c + SLOTS, slot, SLOTS))
                    if is_tile(c, 0):
                        pe.wait_ge(src_in[slot], 16 * since(i, c + SLOTS, slot, SLOTS))
                    for m in range(CH + 1 if is_tile(c, 0) else CH):
                        last = pe.transpose(XT[:, cols(m, m + 1)], rows[:, slot, m, :], ident[:, :])
                    last.then_inc(S["pe_a"], 1)
                if is_group(c, 6):
                    pe.wait_ge(S["act_c"], s - 5)
                    need(pe, S["act_o"], s - 7)
                    pe.matmul(Y[b], ones3[:, :], bias3[:, 1, :], start=True, stop=False, skip_group_check=True)
                    for m in range(CH):
                        last = pe.matmul(Y[b][:, cols(m, m + 1)], x1T[:, 1 - b, m, :], w_cen[:, W_ROOT, :],
                                         start=False, stop=True, skip_group_check=True)
                    last.then_inc(S["pe_d"], 1)

            run_steps(pe, PLAN_A, step)

            pe.wait_ge(S["act_o"], GROUPS)
            pe.wait_ge(S["dve_scan"], TILES)
            pe.wait_ge(S["dve_t"], GROUPS)
            pe.wait_ge(S["deg_dve"], 1)
            pe.matmul(GT[0:1, 0:TILES], seg[:, 1, P - 1:P], ident[0:TILES, 0:TILES], start=True, stop=True)
            pe.matmul(GT[0:1, P:P + TILES], seg[:, 2, P - 1:P], ident[0:TILES, 0:TILES], start=True, stop=True) \
                .then_inc(S["deg_pe"], 1)
            pe.wait_ge(S["deg_dve"], 2)
            pe.matmul(GT[0:TILES, 0:1], carry[0:1, 2, 0:TILES], one[0:1, 0:1], start=True, stop=True) \
                .then_inc(S["deg_pe"], 1)
            pe.wait_ge(S["deg_dve"], 3)
            pe.transpose(GT[:, 0:TILES], seg[:, 4, :], ident[0:TILES, 0:TILES]).then_inc(S["deg_pe"], 1)
            pe.wait_ge(S["deg_dve"], 4)

            def step_c(i, c):
                s = SLOTS * i + c
                slot, b = c % SLOTS, c % 2
                if 0 <= c - 4 < PAIRS:
                    pe.wait_ge(S["dve_sum"], s - 3)
                    need(pe, S["dve_r"], 2 * (s - 4) if isinstance(s, int) and s == 4 else s - 4)
                    for n in range(PAIR):
                        last = pe.transpose(ST[:, cols(n, n + 1)], sums[:, b, n, :], ident[:, :])
                    last.then_inc(S["pe_s"], 1)
                if c < PAIRS:
                    need(pe, S["act_g"], s)
                    pe.wait_ge(x1_in[slot], 16 * PAIR * since(i, c + SLOTS, slot, SLOTS))
                    for n in range(PAIR):
                        last = pe.transpose(GT[:, cols(n, n + 1)], rows[:, slot, n, :], ident[:, :])
                    last.then_inc(S["pe_g"], 1)
                if 0 <= c - 2 < PAIRS:
                    pe.wait_ge(S["dve_prod"], PAIR * (s - 1))
                    need(pe, S["dve_sum"], s - 4)
                    for m in range(NB):
                        last = pe.matmul(MT[b][:, 0:PAIR * D], w_cen[:, W_BASE + m, :],
                                         prod[:, b, m, :, :].rearrange("p t d -> p (t d)"),
                                         start=(m == 0), stop=(m == NB - 1))
                    last.then_inc(S["pe_m"], 1)
                if c < PAIRS:
                    for n in range(PAIR):
                        need(pe, S["dve_prod"], PAIR * (s - 1) + n + 1)
                        for m in range(NB):
                            last = pe.matmul(CB[n][:, cols(m, m + 1)], comp_rep[:, m, :],
                                             onehot[:, bass.ds((s * PAIR + n) * P, P)], start=True, stop=True,
                                             skip_group_check=True)
                        last.then_inc(S["pe_cb"], 1)

            run_steps(pe, PLAN_C, step_c)

        @block.scalar
        def _(act):
            for tile, ap in ((src_i, src_cols), (dst_i, dst_cols), (dst_n, dst_next_cols), (e_weight, weight_cols),
                             (d_cur, dst_rows), (d_prev, dst_prev_rows)):
                act.dma_start(tile[:, :], ap).then_inc(S["edges_in"], 16)
            act.dma_start(soft[:, 0:1], coeff_raw.broadcast_to([P, 1])).then_inc(S["weights_in"], 16)
            for k in range(PARTS):
                act.dma_start(comp_raw[k * REL:(k + 1) * REL, :], comp).then_inc(S["weights_in"], 16)
            act.wait_ge(S["soft_dve"], 1)
            nc.scalar.activation(soft[:, 2:3], soft[:, 1:2], ACT.Exp, scale=-1.0).then_inc(S["soft_act"], 1)
            act.wait_ge(S["soft_act"], 1)
            nc.scalar.activation(soft[:, 3:4], soft[:, 2:3], ACT.Ln, bias=1.0).then_inc(S["soft_act"], 1)

            def step(i, c):
                s = SLOTS * i + c
                b = c % 2
                if is_group(c, 5):
                    act.wait_ge(S["pe_c"], s - 4)
                    need(act, S["pe_d"], s - 6)
                    nc.scalar.copy(x1T[:, b, :, :].rearrange("p c d -> p (c d)"), VT).then_inc(S["act_c"], 1)
                if is_group(c, 0):
                    act.wait_ge(S["pe_a"], s + 1)
                    need(act, S["pe_b"], s - 1)
                    if is_tile(c, 2):
                        act.wait_ge(S["pe_e"], s - 1)
                    n = CH + 1 if is_tile(c, 0) else CH
                    if not is_dense(c, 0):
                        act.wait_ge(S["dve_scan"], TILES - 2 if c < DENSE + 2 else TILES)
                        nc.scalar.copy(agg_now[:, b, :, :], agg_all[:, bass.ds((s - DENSE) * CH, CH), :])
                    nc.scalar.copy(xT[:, b, 0:n, :].rearrange("p c d -> p (c d)"), XT[:, cols(0, n)]) \
                        .then_inc(S["act_a"], 1)
                if 1 <= c <= GROUPS + 3:
                    act.wait_ge(S["dve_q"], s)
                    if is_group(c, 8):
                        act.wait_ge(S["act_o"], s - 7)
                    nc.scalar.activation(st[:, 7, :], st[:, 6, :], ACT.Sqrt).then_inc(S["act_q"], 1)
                if is_group(c, 4):
                    act.wait_ge(S["dve_m"], s - 3)
                    need(act, S["pe_c"], s - 5)
                    if is_dense(c, 6):
                        act.wait_ge(x1_stored[b], 16 * since(i, c, 4 + b, 2))
                    elif is_group(c, 6):
                        act.wait_ge(x1_scattered[b], 16 * CH * since(i, c, DENSE + 4 + (b + DENSE + 4) % 2, 2))
                    for m in range(CH):
                        last = nc.scalar.activation(x1[:, b, m, :], hn[:, (c - 4) % SLOTS, m, :], ACT.Identity,
                                                    bias=st[:, 3, m:m + 1], scale=st[:, 7, RES + m:RES + m + 1])
                    last.then_inc(S["act_x"], 1)
                if is_dense(c, 6):
                    act.wait_ge(S["pe_d"], s - 5)
                    need(act, S["dve_q"], s - 1)
                    for m in range(CH):
                        last = nc.scalar.activation(junk[:, b, m, :], Y[b][:, cols(m, m + 1)], ACT.Square,
                                                    accum_out=ysq[:, b, m:m + 1])
                    last.then_inc(S["act_y"], 1)
                if is_dense(c, 7):
                    act.wait_ge(S["act_q"], s)
                    if c >= 9:
                        act.wait_ge(out_stored[b], 16 * since(i, c, 8 - b, 2))
                    for m in range(CH):
                        last = nc.scalar.activation(outb[:, b, m, :], Y[1 - b][:, cols(m, m + 1)], ACT.Copy,
                                                    scale=st[:, 7, ROOT + m:ROOT + m + 1])
                    last.then_inc(S["act_o"], 1)
                elif is_group(c, 7):
                    act.wait_ge(S["pe_d"], s - 6)
                    nc.scalar.copy(y_root[:, bass.ds((s - 7 - DENSE) * CH * D, CH * D)], Y[1 - b]) \
                        .then_inc(S["act_o"], 1)

            run_steps(act, PLAN_A, step)

            def step_c(i, c):
                s = SLOTS * i + c
                b = c % 2
                if c < PAIRS:
                    act.wait_ge(S["pe_g"], s + 1)
                    need(act, S["dve_prod"], PAIR * (s - 1))
                    nc.scalar.copy(xT[:, b, 0:PAIR, :].rearrange("p c d -> p (c d)"), GT[:, 0:PAIR * D]) \
                        .then_inc(S["act_g"], 1)
                if 0 <= c - 4 < PAIRS:
                    act.wait_ge(S["dve_r"], s - 3)
                    need(act, S["act_out"], s - 4)
                    nc.scalar.activation(st[:, 7, 0:PAIR], st[:, 6, 0:PAIR], ACT.Sqrt).then_inc(S["act_r"], 1)
                    act.wait_ge(S["act_r"], s - 3)
                    if c >= 8:
                        act.wait_ge(out_scattered[c % SLOTS], 16 * PAIR * since(i, c, 4 + c % SLOTS, SLOTS))
                    for n in range(PAIR):
                        last = nc.scalar.activation(outb[:, b, PAIR * (c // 2 % 2) + n, :], y_rows[:, b, n, :],
                                                    ACT.Copy, scale=st[:, 7, n:n + 1])
                    last.then_inc(S["act_out"], 1)

            run_steps(act, PLAN_C, step_c)

        @block.vector
        def _(dve):
            own = Chain(dve, S["dve_own"])

            own.mark(dve.memset(bn[:, :, :], 0.0))
            own.mark(dve.memset(ysq[:, :, :], 0.0))
            own.mark(dve.memset(st[:, :, :], 0.0))
            dve.wait_ge(S["weights_in"], 16 * N_W)
            dve.wait_ge(S["ident_ready"], 1)
            own.link(dve.tensor_tensor(w_raw[:, W_ROOT, :], w_raw[:, W_ROOT, :], ident[:, :], ALU.add))
            own.link(dve.tensor_reduce(row_mean[:, 0:12], w_raw[:, :, :], AX_X, ALU.add))
            own.link(dve.tensor_scalar(row_mean[:, 0:12], row_mean[:, 0:12], 1.0 / D, None, ALU.mult))
            own.mark(dve.tensor_tensor(w_cen[:, :, :], w_raw[:, :, :],
                                       row_mean[:, 0:12].unsqueeze(2).broadcast_to([P, 12, D]), ALU.subtract))
            own.link(dve.tensor_reduce(row_mean[:, 12:15], vec_raw[:, 0:3, :], AX_X, ALU.add))
            own.link(dve.tensor_scalar(row_mean[:, 12:15], row_mean[:, 12:15], 1.0 / D, None, ALU.mult))
            own.link(dve.tensor_tensor(vec_cen[:, :, :], vec_raw[:, 0:3, :],
                                       row_mean[:, 12:15].unsqueeze(2).broadcast_to([P, 3, D]), ALU.subtract))
            dve.wait_ge(S["const_ready"], N_CONST)
            both = vec_cen[0:PARTS, 0:2, :].rearrange("p v d -> p (v d)")
            for k in range(PARTS):
                own.mark(dve.tensor_scalar(part_mask[:, 0, k:k + 1], part_id[:, :], float(k), None, ALU.is_equal))
            own.mark(dve.tensor_scalar(part_mask[:, 1, 0:1], part_id[:, :], float(REL), None, ALU.is_lt))
            own.mark(dve.tensor_scalar(part_mask[:, 1, 2:3], part_id[:, :], float(2 * REL), None, ALU.is_ge))
            own.link(dve.tensor_scalar(part_mask[:, 1, 1:2], part_id[:, :], float(REL), None, ALU.is_ge))
            own.mark(dve.tensor_tensor(part_mask[:, 1, 1:2], part_mask[:, 1, 1:2], part_mask[:, 1, 2:3],
                                       ALU.subtract))

            def split3(value, parts, rem, masks, n):
                own.link(dve.tensor_copy(parts[0], value))
                own.link(dve.tensor_tensor(rem[0], value, parts[0], ALU.subtract))
                own.link(dve.tensor_copy(parts[1], rem[0]))
                own.link(dve.tensor_tensor(rem[1], rem[0], parts[1], ALU.subtract))
                own.link(dve.tensor_copy(parts[2], rem[1]))
                own.link(dve.tensor_scalar(rem[0], parts[0], masks[0:n, 0:1], None, ALU.mult))
                for k in range(1, PARTS):
                    own.link(dve.scalar_tensor_tensor(rem[0], parts[k], masks[0:n, k:k + 1], rem[0],
                                                      ALU.mult, ALU.add))

            split3(both, [split[:, k, :] for k in range(PARTS)], [rest[:, k, :] for k in range(2)],
                   part_mask[:, 0, :], PARTS)
            for v in range(2):
                own.mark(dve.tensor_copy(bias3[:, v, :].rearrange("p (c d) -> p c d", c=CH),
                                         rest[:, 0:1, cols(v, v + 1)].broadcast_to([PARTS, CH, D])))
            own.link(dve.tensor_scalar(soft[:, 4:5], soft[:, 0:1], -1.0, None, ALU.mult))
            dve.tensor_tensor(soft[:, 1:2], soft[:, 0:1], soft[:, 4:5], ALU.max).then_inc(S["soft_dve"], 1)
            K3 = PARTS * REL
            split3(comp_raw[:, :], [comp_split[:, k, :] for k in range(PARTS)],
                   [comp_rest[:, k, :] for k in range(2)], part_mask[:, 1, :], K3)
            own.mark(dve.tensor_copy(comp_rep[:, :, :], comp_rest[:, 0, :].unsqueeze(2).broadcast_to([K3, NB, P])))
            dve.wait_ge(S["soft_act"], 2)
            own.link(dve.tensor_scalar(soft[:, 5:6], soft[:, 0:1], 0.0, soft[:, 3:4], ALU.max, ALU.add))
            dve.wait_ge(S["edges_in"], 16 * N_EDGE)
            own.mark(dve.tensor_scalar(e_scale[:, :], e_weight[:, :], soft[:, 5:6], 1.0, ALU.mult, ALU.add))
            own.link(dve.tensor_tensor(same_next[:, :], dst_i[:, :], dst_n[:, :], ALU.is_equal))
            dve.scalar_tensor_tensor(scat_i[:, :], same_next[:, :], float(SKIP), dst_i[:, :],
                                     ALU.mult, ALU.add).then_inc(S["scat_ready"], 1)

            def masks(a, b):
                return dve.tensor_tensor(same_prev[:, a:b], line[:, a + 1:b + 1], line[:, a:b], ALU.is_equal)

            dve.wait_ge(S["line_in"], 16)
            masks(0, FIRST_LINE).then_inc(S["setup_dve"], 1)
            dve.wait_ge(S["setup_dve"], 1)

            def moments(a, b):
                me, m2e, mo, m2o = (bn[:, a:b, k] for k in (1, 2, 4, 5))
                own.mark(dve.tensor_tensor(st[:, 0, a:b], me, mo, ALU.subtract))
                return own.mark(dve.tensor_tensor(st[:, 1, a:b], m2e, m2o, ALU.add))

            def spread(a, b):
                own.mark(dve.scalar_tensor_tensor(st[:, 2, a:b], st[:, 0, a:b], 0.25, st[:, 0, a:b],
                                                  ALU.mult, ALU.mult))
                return own.mark(dve.tensor_scalar(st[:, 1, a:b], st[:, 1, a:b], 1.0 / D, LN_EPS, ALU.mult, ALU.add))

            def step(i, c):
                s = SLOTS * i + c
                b = c % 2
                if c == 4:
                    dve.wait_ge(S["line_rest_in"], 16)
                    own.link(masks(FIRST_LINE, EP))
                if is_group(c, 1):
                    dve.wait_ge(S["pe_b"], s)
                    for m in range(CH):
                        own.mark(dve.bn_stats(bn[:, m, :], H[1 - b][:, cols(m, m + 1)]))
                if is_tile(c, 1):
                    dve.wait_ge(S["pe_e"], s)
                    hp_at = own.mark(dve.scalar_tensor_tensor(hp[:, :], HE, e_scale[:, bass.ds(s - 1, 1)],
                                                              vec_cen[:, 2, :], ALU.mult, ALU.add))
                if is_tile(c, 2):
                    dve.wait_ge(S["pe_cp"], s - 1)
                    need(dve, S["dve_scan"], s - 2)
                    first = 0.0 if c == 2 else agg_line[:, bass.ds((s - 2) * P - 1, 1)]
                    dve.tensor_tensor_scan(agg_line[:, bass.ds((s - 2) * P, P)], same_prev[:, bass.ds((s - 2) * P, P)],
                                           PT, first, ALU.mult, ALU.max).then_inc(S["dve_scan"], 1)
                if is_tile(c, 1):
                    own.need(hp_at)
                    own.mark(dve.bn_stats(bn[:, SRC, :], hp[:, :]))

                def residual_stats(a, z):
                    if is_group(c, 3):
                        if a == 0:
                            dve.wait_ge(S["dve_v"], s - 2)
                        for m in range(a, z):
                            own.mark(dve.bn_stats(bn[:, RES + m, :], hn[:, (c - 3) % SLOTS, m, :]))

                if 1 <= c <= GROUPS + 3:
                    own.need(own.count)
                    at = moments(0, ROOT)
                    if is_group(c, 4):
                        need(dve, S["dve_m"], s - 4)
                        at = own.mark(dve.tensor_tensor(st[:, 3, RES:ROOT], bn[:, RES:ROOT, 1], bn[:, RES:ROOT, 4],
                                                        ALU.add))
                    own.need(at)
                    at = spread(0, ROOT)
                    if is_dense(c, 7):
                        dve.wait_ge(S["act_y"], s - 6)
                        own.mark(dve.tensor_scalar(st[:, 5, ROOT:ROOT + CH], ysq[:, 1 - b, :], 1.0 / D, LN_EPS,
                                                   ALU.mult, ALU.add))
                    residual_stats(0, 1)
                    own.need(at)
                    at = own.mark(dve.tensor_tensor(st[:, 5, 0:ROOT], st[:, 2, 0:ROOT], st[:, 1, 0:ROOT], ALU.add))
                    residual_stats(1, 2)
                    own.need(at)
                    n = ROOT + CH if is_dense(c, 7) else ROOT
                    dve.reciprocal(st[:, 6, 0:n], st[:, 5, 0:n]).then_inc(S["dve_q"], 1)
                residual_stats(2, CH)
                if is_group(c, 2):
                    dve.wait_ge(S["pool_b"], s - 1)
                    h = hn[:, (c - 2) % SLOTS, :, :].rearrange("p c d -> p (c d)")
                    dve.scalar_tensor_tensor(
                        h, h, 0.0, rows[:, (c - 2) % SLOTS, 0:CH, :].rearrange("p c d -> p (c d)"),
                        ALU.max, ALU.add).then_inc(S["dve_v"], 1)
                if 1 <= c <= GROUPS + 3:
                    dve.wait_ge(S["act_q"], s)
                if is_group(c, 4):
                    dve.scalar_tensor_tensor(st[:, 3, 0:CH], st[:, 3, RES:ROOT], -0.5, st[:, 7, RES:ROOT],
                                             ALU.mult, ALU.mult).then_inc(S["dve_m"], 1)
                if is_group(c, 1):
                    if is_tile(c, 1):
                        need(dve, S["pe_cp"], s - 2)
                        dve.scalar_tensor_tensor(pooled[:, b, :], hp[:, :], st[:, 7, SRC:SRC + 1],
                                                 vec_raw[:, GAM_P, :], ALU.mult, ALU.mult).then_inc(S["dve_te"], 1)
                    need(dve, S["act_x"], s - 4)
                    for m in range(CH):
                        last = dve.scalar_tensor_tensor(hn[:, (c - 1) % SLOTS, m, :], H[1 - b][:, cols(m, m + 1)],
                                                        st[:, 7, m:m + 1], vec_raw[:, GAM_F, :],
                                                        ALU.mult, ALU.mult)
                        if m < CH - 1:
                            own.mark(last)
                    last.then_inc(S["dve_t"], 1)

            run_steps(dve, PLAN_A, step, own, (SLOTS * 20, SLOTS * 17))

            own = Chain(dve, S["c_own"])
            own.link(dve.tensor_scalar(rel_id[:, :], part_mask[0:K3, 1, 1:2], -float(REL), part_id[0:K3, :],
                                       ALU.mult, ALU.add))
            own.link(dve.scalar_tensor_tensor(rel_id[:, :], part_mask[0:K3, 1, 2:3], -float(2 * REL), rel_id[:, :],
                                              ALU.mult, ALU.add))

            same, pos, run, deg = (seg[:, k, :] for k in (0, 1, 2, 3))
            own.link(dve.tensor_tensor(same, d_cur[:, :], d_prev[:, :], ALU.is_equal))
            own.mark(dve.tensor_tensor_scan(run, same, same, 1.0, ALU.mult, ALU.min))
            own.link(dve.tensor_copy(deg, same))
            own.link(dve.memset(deg[:, 0:1], 0.0))
            own.link(dve.tensor_tensor_scan(pos, deg, deg, 0.0, ALU.mult, ALU.add))
            dve.tensor_scalar(seg[:, 4, 0:1], pos[:, 0:1], 1.0, None, ALU.add).then_inc(S["deg_dve"], 1)
            dve.wait_ge(S["deg_pe"], 1)
            own.mark(dve.tensor_scalar(carry[:, 0, 0:TILES], GT[0:1, 0:TILES], 1.0, None, ALU.add))
            own.link(dve.tensor_copy(carry[:, 1, 0:TILES], GT[0:1, P:P + TILES]))
            dve.tensor_tensor_scan(carry[:, 2, 1:TILES], carry[:, 1, 0:TILES - 1], carry[:, 0, 0:TILES - 1], 0.0,
                                   ALU.mult, ALU.add).then_inc(S["deg_dve"], 1)
            dve.wait_ge(S["deg_pe"], 2)
            own.link(dve.tensor_copy(carry_col[:, :], GT[0:TILES, 0:1]))
            own.link(dve.scalar_tensor_tensor(pos, run, carry_col[:, 0:1], pos, ALU.mult, ALU.add))
            own.link(dve.tensor_scalar(deg, pos, 1.0, None, ALU.add))
            dve.reciprocal(seg[:, 4, :], deg).then_inc(S["deg_dve"], 1)
            dve.wait_ge(S["deg_pe"], 3)
            own.link(dve.tensor_copy(inv_deg[:, :], GT[:, 0:TILES]))
            dve.wait_ge(S["types_in"], 16)
            dve.tensor_scalar(onehot[:, :], types[0:K3, 0:EP], rel_id[:, 0:1], None,
                              ALU.is_equal).then_inc(S["deg_dve"], 1)

            def step_c(i, c):
                s = SLOTS * i + c
                b = c % 2
                last_pair = 0 <= c - 4 < PAIRS

                def product(n):
                    if 0 <= c - 1 < PAIRS:
                        dve.wait_ge(S["pe_cb"], PAIR * (s - 1) + n + 1)
                        if n == 0:
                            dve.wait_ge(S["act_g"], s)
                            need(dve, S["pe_m"], s - 3)
                        dve.tensor_tensor(prod[:, 1 - b, :, n, :], CB[n].rearrange("p (m d) -> p m d", m=NB),
                                          xT[:, 1 - b, n:n + 1, :].broadcast_to([P, NB, D]), ALU.mult) \
                           .then_inc(S["dve_prod"], 1)

                if last_pair:
                    dve.wait_ge(S["pe_s"], s - 3)
                    need(dve, S["act_out"], s - 5)
                    for n in range(PAIR):
                        t = (s - 4) * PAIR + n
                        own.mark(dve.scalar_tensor_tensor(y_rows[:, b, n, :], ST[:, cols(n, n + 1)],
                                                          inv_deg[:, bass.ds(t, 1)], y_root[:, bass.ds(t * D, D)],
                                                          ALU.mult, ALU.add))
                    own.need(own.count)
                    for n in range(PAIR):
                        at = own.mark(dve.bn_stats(bn[:, n, :], y_rows[:, b, n, :]))
                product(0)
                if last_pair:
                    own.need(at)
                    at = moments(0, PAIR)
                if 0 <= c - 3 < PAIRS:
                    dve.wait_ge(S["pe_m"], s - 2)
                    need(dve, S["pe_s"], s - 4)
                    need(dve, S["dve_sum"], s - 3)
                    first = 0.0 if c == 3 else sums[:, b, PAIR - 1, D - 1:D]
                    dve.tensor_tensor_scan(sums[:, 1 - b, :, :].rearrange("p t d -> p (t d)"),
                                           same_prev[:, bass.ds((s - 3) * PAIR * P, PAIR * P)],
                                           MT[1 - b][:, 0:PAIR * D], first, ALU.mult, ALU.add) \
                       .then_inc(S["dve_sum"], 1)
                if last_pair:
                    own.need(at)
                    at = spread(0, PAIR)
                product(1)
                if last_pair:
                    own.need(at)
                    own.link(dve.tensor_tensor(st[:, 5, 0:PAIR], st[:, 2, 0:PAIR], st[:, 1, 0:PAIR], ALU.add))
                    need(dve, S["act_r"], s - 4)
                    dve.reciprocal(st[:, 6, 0:PAIR], st[:, 5, 0:PAIR]).then_inc(S["dve_r"], 1)

            run_steps(dve, PLAN_C, step_c, own, (SLOTS * 9,))


def kernel(x, src, dst, edge_type_16, edge_weight, L0_gnn_pool_w, L0_gnn_pool_b, L0_gnn_ln_pool_g,
           L0_gnn_ln_pool_b, L0_gnn_final_w, L0_gnn_final_b, L0_gnn_ln_final_g, L0_gnn_ln_final_b,
           L0_gnn_coeff_raw, L1_gnn_weight, L1_gnn_comp, L1_gnn_bias):
    import numpy as np
    import concourse.bacc as bacc
    from concourse.bass_utils import run_bass_kernel_spmd

    x, src, dst, edge_type, edge_weight = (np.asarray(a) for a in (x, src, dst, edge_type_16, edge_weight))
    N, E = x.shape[0], src.shape[0]
    tiles = -(-E // P)

    def line(a, fill, extra=0):
        return np.concatenate([a, np.full(tiles * P + extra - E, fill, a.dtype)])

    def by_tile(a):
        return np.ascontiguousarray(a.reshape(tiles, P).T)

    dst_ext = line(dst, N, 1)
    arrays = {
        "x": x,
        "src_cols": by_tile(line(src, 0)),
        "dst_cols": by_tile(dst_ext[:-1]),
        "dst_next_cols": by_tile(dst_ext[1:]),
        "dst_rows": dst_ext[:-1].reshape(tiles, P),
        "dst_prev_rows": np.concatenate([np.full(1, -1, dst.dtype), dst_ext[:-2]]).reshape(tiles, P),
        "dst_line": np.concatenate([np.full(1, -1, dst.dtype), dst_ext[:-1]])[None, :],
        "type_line": line(edge_type, 0)[None, :],
        "weight_cols": by_tile(line(edge_weight, 0)),
        "pool_w": L0_gnn_pool_w, "pool_b": L0_gnn_pool_b, "ln_pool_g": L0_gnn_ln_pool_g,
        "ln_pool_b": L0_gnn_ln_pool_b, "final_w": L0_gnn_final_w, "final_b": L0_gnn_final_b,
        "ln_final_g": L0_gnn_ln_final_g, "ln_final_b": L0_gnn_ln_final_b, "coeff_raw": L0_gnn_coeff_raw,
        "weight": L1_gnn_weight, "comp": L1_gnn_comp, "bias": L1_gnn_bias,
    }
    nc = bacc.Bacc("TRN2", target_bir_lowering=False, num_devices=1)
    feed, aps = {}, {}
    for name, a in arrays.items():
        a = np.asarray(a)
        a = np.ascontiguousarray(a.reshape(1, -1) if a.ndim < 2 else a)
        feed[f"in_{name}"] = a
        aps[name] = nc.dram_tensor(f"in_{name}", a.shape, mybir.dt.from_np(a.dtype), kind="ExternalInput").ap()
    aps["out"] = nc.dram_tensor("out_rows", x.shape, F32, kind="ExternalOutput").ap()
    gnn_kernel(nc, **aps)
    r = run_bass_kernel_spmd(nc, [feed], core_ids=[0])
    return r.results[0]["out_rows"]
```

```python
from contextlib import ExitStack

import concourse.bass as bass
from concourse import mybir

P = 128
CH = 4
SRC = CH
NB = 8
REL = 16
PARTS = 3
LN_EPS = 1e-5
SKIP = 1 << 20
SLOTS = 4
UNROLL = 2 * SLOTS
PAIR = 2

ALU = mybir.AluOpType
ACT = mybir.ActivationFunctionType
F32 = mybir.dt.float32
BF16 = mybir.dt.bfloat16
I32 = mybir.dt.int32
U32 = mybir.dt.uint32
U8 = mybir.dt.uint8
AX_X = mybir.AxisListType.X


def need(eng, sem, count):
    if isinstance(count, int) and count <= 0:
        return
    eng.wait_ge(sem, count)


class Chain:

    def __init__(self, eng, sem):
        self.eng, self.sem, self.count, self.base = eng, sem, 0, 0

    def mark(self, ins):
        ins.then_inc(self.sem, 1)
        self.count += 1
        return self.count

    def need(self, at):
        self.eng.wait_ge(self.sem, self.base + at)

    def link(self, ins):
        self.need(self.mark(ins))


def run_steps(eng, plan, step, chain=None, marks=()):
    marks = list(marks)
    for first, last, unrolled in plan:
        if not unrolled:
            for s in range(first, last + 1):
                step(0, s)
            continue
        assert first % SLOTS == 0 and unrolled % SLOTS == 0 and (last - first + 1) % unrolled == 0
        loops = (last - first + 1) // unrolled
        with eng.Fori(0, loops) as i:
            if chain:
                before, base, per_pass = chain.count, chain.base, unrolled * marks.pop(0)
                chain.base = i * per_pass + base
            for c in range(first, first + unrolled):
                step(i * (unrolled // SLOTS), c)
        if chain:
            assert chain.count - before == per_pass, ("marks in a pass", chain.count - before)
            chain.base = base + (loops - 1) * per_pass


def gnn_kernel(nc, x, src_cols, dst_cols, dst_next_cols, dst_rows, dst_prev_rows, type_line,
               weight_cols, pool_w, pool_b, ln_pool_g, ln_pool_b, final_w, final_b, ln_final_g, ln_final_b,
               coeff_raw, weight, comp, bias, out):
    N, D = x.shape
    TILES = src_cols.shape[1]
    EP = TILES * P
    ROWS = CH * P
    DENSE = -(-N // ROWS)
    TAIL = (N - (DENSE - 1) * ROWS) // CH
    EDGE = -(-TILES // CH)
    GROUPS = DENSE + EDGE
    LAST_TILES = TILES - (EDGE - 1) * CH
    PAIRS = TILES // PAIR
    assert DENSE == TILES and D == P and (N - (DENSE - 1) * ROWS) % CH == 0 and TILES % PAIR == 0

    LAST_A = GROUPS + 6
    LOOP_A = 2 * SLOTS
    LOOP_A_END = LOOP_A + (DENSE - 2 - LOOP_A) // UNROLL * UNROLL
    LOOP_E = -(-(DENSE + 7) // SLOTS) * SLOTS
    LOOP_E_END = LOOP_E + (GROUPS - 1 - LOOP_E) // SLOTS * SLOTS
    PLAN_A = [(0, LOOP_A - 1, 0), (LOOP_A, LOOP_A_END - 1, UNROLL), (LOOP_A_END, LOOP_E - 1, 0),
              (LOOP_E, LOOP_E_END - 1, SLOTS), (LOOP_E_END, LAST_A, 0)]
    LAST_C = PAIRS + 3
    LOOP_C = 2 * SLOTS
    LOOP_C_END = LOOP_C + (PAIRS - 2 - LOOP_C) // UNROLL * UNROLL
    PLAN_C = [(0, LOOP_C - 1, 0), (LOOP_C, LOOP_C_END - 1, UNROLL), (LOOP_C_END, LAST_C, 0)]

    x1_table = nc.dram_tensor("x1_table", [N, D], F32).ap()
    mask_line = nc.dram_tensor("mask_line", [1, TILES * P], U8).ap()
    x_dst_table = nc.dram_tensor("x_dst_table", [P, TILES * D], F32).ap()

    with ExitStack() as ctx:
        def sb(name, shape, dt=F32):
            return ctx.enter_context(nc.sbuf_tensor(name, shape, dt))

        def sem(name):
            return ctx.enter_context(nc.semaphore(name))

        ident = sb("ident", [P, P])
        part_id = sb("part_id", [P, 1])
        row_mean = sb("row_mean", [P, 16])
        w_cen = sb("w_cen", [P, 13, D])
        vec_raw = sb("vec_raw", [P, 7, D])
        vec_cen = sb("vec_cen", [P, 3, D])
        bias3 = sb("bias3", [PARTS, 3, CH * D], BF16)
        ones3 = sb("ones3", [PARTS, P], BF16)
        comp_raw = sb("comp_raw", [PARTS * REL, NB])
        comp_split = sb("comp_split", [PARTS * REL, PARTS, NB], BF16)
        comp_rest = sb("comp_rest", [PARTS * REL, 2, NB])
        comp_rep = sb("comp_rep", [PARTS * REL, NB, P], BF16)
        part_mask = sb("part_mask", [P, 2, PARTS])
        rel_id = sb("rel_id", [PARTS * REL, 1])
        one = sb("one", [P, 1])
        soft = sb("soft", [P, 7])
        src_i = sb("src_i", [P, TILES], I32)
        dst_i = sb("dst_i", [P, TILES], I32)
        dst_n = sb("dst_n", [P, TILES], I32)
        scat_i = sb("scat_i", [P, TILES], I32)
        idx = sb("idx", [P, SLOTS, CH], I32)
        same_next = sb("same_next", [P, TILES])
        e_scale = sb("e_scale", [P, TILES])
        e_weight = sb("e_weight", [P, TILES])
        inv_deg = sb("inv_deg", [P, TILES])
        same_prev = sb("same_prev", [P, EP], U8)
        onehot = sb("onehot", [PARTS * REL, EP], BF16)
        d_cur = sb("d_cur", [TILES, P], I32)
        d_prev = sb("d_prev", [TILES, P], I32)
        carry = sb("carry", [1, 3, P])
        carry_col = sb("carry_col", [TILES, 1])
        same_rows = sb("same_rows", [TILES, P], U8)
        rows = sb("rows", [P, SLOTS, CH + 1, D])
        x_dst = sb("x_dst", [P, SLOTS, D])
        xT = sb("xT", [P, 2, CH + 1, D])
        hp = sb("hp", [P, D])
        pooled = sb("pooled", [P, 2, D])
        work = sb("work", [P, 8 * CH, D])
        agg_now = sb("agg_now", [P, 2, CH, D])
        outb = sb("outb", [P, 2, CH, D])
        junk = sb("junk", [P, 2, CH, D], BF16)
        bn = sb("bn", [P, 2 * CH + 1, 6])
        st = sb("st", [P, 8, 3 * CH + 1])
        ysq = sb("ysq", [P, 2, CH])
        agg_all = sb("agg_all", [P, EDGE * CH, D])
        y_root = sb("y_root", [P, EDGE * CH * D])

        w_raw = y_root[:, 0:12 * D].rearrange("p (w d) -> p w d", w=12)
        zero = hp
        x1 = work[:, 0:2 * CH, :].rearrange("p (b c) d -> p b c d", b=2)
        x1T = work[:, 2 * CH:4 * CH, :].rearrange("p (b c) d -> p b c d", b=2)
        hn = work[:, 4 * CH:8 * CH, :].rearrange("p (b c) d -> p b c d", b=4)
        agg_line = agg_all[:, :, :].rearrange("p t d -> p (t d)")
        types = agg_line.bitcast(I32)
        biases, rest = outb[0:PARTS, 0, 0:3, :], outb[0:PARTS, 1, :, :]
        split = x1[0:PARTS, :, :, :].rearrange("p b c d -> p (b c d)").bitcast(BF16)
        seg = agg_now[0:TILES, :, :, :].rearrange("p b c d -> p (b c) d")
        prod = work[:, :, :].rearrange("p (b m t) d -> p b m t d", b=2, m=NB)
        sums = agg_now[:, 0, :, :].rearrange("p (b t) d -> p b t d", b=2)
        y_rows = agg_now[:, 1, :, :].rearrange("p (b t) d -> p b t d", b=2)

        ps = ctx.enter_context(nc.psum_tensor("ps", [P, 8, 512], F32))

        def banks(a, n):
            return ps[:, a:a + n, :].rearrange("p b n -> p (b n)")

        XT, H = banks(0, 2), [banks(2, 1), banks(3, 1)]
        HD, HG = H
        VT, HE, PT = banks(4, 1), ps[:, 5, 0:D], ps[:, 5, D:2 * D]
        Y = [banks(6, 1), banks(7, 1)]
        CB = [banks(0, 2), banks(2, 2)]
        GT, MT, ST = banks(4, 1), [banks(5, 1), banks(6, 1)], banks(7, 1)

        names = ("weights_in", "soft_in", "vectors_in", "bases_in", "rows_of_dst_in", "index_in", "edges_in", "mask_made", "mask_stored",
                 "masks_in", "types_in", "onehot", "const_ready", "ident_ready", "scat_ready",
                 "setup_dve", "soft_dve", "soft_act", "pe_a", "act_a", "pe_b", "pe_bg", "pe_e", "dve_h", "dve_q", "act_q", "dve_m",
                 "dve_t", "dve_te", "pool_b", "pool_p", "dve_v", "act_x", "pool_x", "pe_c", "pe_cp", "act_c", "dve_scan", "pe_d",
                 "act_y", "act_o", "dve_own", "idx_ready", "deg_dve", "deg_pe", "c_own", "pe_g", "act_g",
                 "pe_cb", "dve_prod", "pe_m", "dve_y", "dve_sum", "pe_s", "dve_r", "act_r", "act_out")
        S = {n: sem(n) for n in names}

        def sems(name, n):
            return [sem(f"{name}{j}") for j in range(n)]

        rows_in, dst_in, src_in = sems("rows_in", SLOTS), sems("dst_in", SLOTS), sems("src_in", SLOTS)
        dst_stored = sems("dst_stored", SLOTS)
        x1_stored, x1_scattered, out_stored = sems("x1_stored", 2), sems("x1_scattered", 2), sems("out_stored", 2)
        x1_in, out_scattered = sems("x1_in", SLOTS), sems("out_scattered", SLOTS)

        full = (DENSE - 1) * ROWS
        x_groups, x1_groups, out_groups = (
            t[0:full, :].rearrange("(g p c) d -> g p (c d)", p=P, c=CH) for t in (x, x1_table, out))
        x_tail, x1_tail, out_tail = (t[full:N, :].rearrange("(p c) d -> p (c d)", c=CH) for t in (x, x1_table, out))

        W_TOP, W_BOT, W_POOL, W_ROOT, W_BASE, W_GAM = 0, 1, 2, 3, 4, 12
        GAM_F, BET_F, GAM_P, BET_P = 3, 4, 5, 6
        N_CONST = 6
        EARLY = (LOOP_E_END - DENSE) * CH * P
        RES, ROOT = CH + 1, 2 * CH + 1

        def cols(a, b):
            return slice(a * D, b * D)

        def is_group(c, k):
            return 0 <= c - k < GROUPS

        def is_dense(c, k):
            return 0 <= c - k < DENSE

        def pool_shares(c, k):
            return is_dense(c, k)

        def is_tile(c, k):
            return 0 <= c - k < TILES

        def since(i, c, first, every):
            assert (c - first) % every == 0
            return SLOTS // every * i + (c - first) // every

        block = ctx.enter_context(nc.Block())

        @block.sync
        def _(sp):
            def load(i, c):
                g, slot = SLOTS * i + c, c % SLOTS
                flat = rows[:, slot, 0:CH, :].rearrange("p c d -> p (c d)")
                if c == DENSE - 1:
                    into, of = flat[0:TAIL], x_tail
                elif c < DENSE:
                    into, of = flat, x_groups[g]
                elif c == GROUPS - 1:
                    into, of = flat[:, 0:LAST_TILES * D], x_dst_table[:, (g - DENSE) * CH * D:TILES * D]
                else:
                    into, of = flat, x_dst_table[:, bass.ds((g - DENSE) * CH * D, CH * D)]
                sp.dma_start(into, of).then_inc(rows_in[slot], 16)

            for w, ap in ((W_TOP, final_w[0:D, :]), (W_POOL, pool_w), (W_BOT, final_w[D:2 * D, :]),
                          (W_ROOT, weight[NB])):
                sp.dma_start(w_raw[:, w, :], ap).then_inc(S["weights_in"], 16)
            sp.dma_start(vec_raw[:, 2, :], pool_b.broadcast_to([P, D])).then_inc(S["weights_in"], 16)
            load(0, 0)
            sp.dma_start(w_raw[:, W_BASE:W_BASE + NB, :], weight[0:NB].rearrange("b k n -> k b n")) \
                .then_inc(S["bases_in"], 16)

            def step(i, c):
                s = SLOTS * i + c
                b = c % 2
                if is_group(c, -1) and c + 1 < DENSE - 1:
                    need(sp, S["dve_v"], s - 2)
                    load(i, c + 1)
                if c == 0:
                    sp.wait_ge(S["mask_made"], 1)
                    sp.dma_start(mask_line.rearrange("o (t e) -> (o t) e", e=P), same_rows[:, :]).then_inc(S["mask_stored"], 16)
                    sp.wait_ge(S["mask_stored"], 16)
                    sp.dma_start(same_prev[:, :], mask_line.broadcast_to([P, EP])).then_inc(S["masks_in"], 16)
                if is_tile(c, 0):
                    slot = c % SLOTS
                    sp.wait_ge(dst_in[slot], 16 * since(i, c + SLOTS, slot, SLOTS))
                    sp.dma_start(x_dst_table[:, bass.ds(s * D, D)], x_dst[:, slot, :]).then_inc(dst_stored[slot], 16)
                if c + 1 in (DENSE, DENSE + 2):
                    for j in range(SLOTS):
                        sp.wait_ge(dst_stored[j], 16 * (len(range(j, TILES, SLOTS)) - (c + 1 == DENSE)))
                if is_group(c, -1) and c + 1 >= DENSE - 1:
                    need(sp, S["dve_v"], s - 2)
                    load(i, c + 1)
                if c == LOOP_E_END:
                    sp.wait_ge(S["act_a"], c)
                    sp.dma_start(types[0:PARTS * REL, 0:EARLY], type_line[:, 0:EARLY].broadcast_to([PARTS * REL, EARLY])) \
                        .then_inc(S["types_in"], 16)
                if c == GROUPS:
                    sp.wait_ge(S["act_a"], GROUPS)
                    sp.dma_start(types[0:PARTS * REL, EARLY:EP], type_line[:, EARLY:EP].broadcast_to([PARTS * REL, EP - EARLY])) \
                        .then_inc(S["types_in"], 16)
                if is_dense(c, 4):
                    sp.wait_ge(S["act_x"], s - 3)
                    sp.wait_ge(S["pool_x"], s - 3)
                    b_ = x1[:, b, :, :].rearrange("p c d -> p (c d)")
                    tail = c - 4 == DENSE - 1
                    sp.dma_start(x1_tail if tail else x1_groups[s - 4], b_[0:TAIL] if tail else b_) \
                        .then_inc(x1_stored[b], 16)
                if is_dense(c, 7):
                    sp.wait_ge(S["act_o"], s - 6)
                    b_ = outb[:, b, :, :].rearrange("p c d -> p (c d)")
                    tail = c - 7 == DENSE - 1
                    sp.dma_start(out_tail if tail else out_groups[s - 7], b_[0:TAIL] if tail else b_) \
                        .then_inc(out_stored[b], 16)

            run_steps(sp, PLAN_A, step)

        @block.gpsimd
        def _(pool):
            for tile, ap in ((d_cur, dst_rows), (d_prev, dst_prev_rows)):
                pool.dma_start(tile[:, :], ap).then_inc(S["rows_of_dst_in"], 16)
            pool.memset(zero[:, :], 0.0).then_inc(S["const_ready"], 1)
            pool.memset(one[:, :], 1.0).then_inc(S["const_ready"], 1)
            pool.memset(ones3[:, :], 1.0).then_inc(S["const_ready"], 1)
            pool.iota(part_id[:, :], [[0, 1]], base=0, channel_multiplier=1,
                      allow_small_or_imprecise_dtypes=True).then_inc(S["const_ready"], 1)
            pool.memset(agg_all[:, TILES:EDGE * CH, :], 0.0).then_inc(S["const_ready"], 1)
            pool.memset(carry[:, :, :], 0.0).then_inc(S["const_ready"], 1)
            pool.wait_ge(S["const_ready"], N_CONST)
            pool.affine_select(out=ident[:, :], in_=zero[:, :], compare_op=ALU.not_equal, fill=1.0, base=0,
                               pattern=[[-1, P]], channel_multiplier=1).then_inc(S["ident_ready"], 1)
            pool.wait_ge(S["index_in"], 16 * 2)
            last_node = pool.to_reg(N - 1)

            def fetch(*pairs):
                for to, of in pairs:
                    pool.tensor_copy(to, of).then_inc(S["idx_ready"], 1)

            def indirect(*args):
                pool.nop(nofuse=True)
                return pool.indirect_dma_start(*args, bounds_check=last_node, oob_is_err=False)

            def by(slot, n):
                return bass.IndirectOffsetOnAxis(ap=idx[:, slot, n:n + 1].bitcast(U32), axis=0)

            def gather_src(i, c):
                t, slot = SLOTS * i + c, c % SLOTS
                fetch((idx[:, slot, 0:1], src_i[:, bass.ds(t, 1)]), (idx[:, slot, 1:2], dst_i[:, bass.ds(t, 1)]))
                pool.wait_ge(S["idx_ready"], 2 * t + 2)
                indirect(rows[:, slot, SRC, :], None, x[:, :], by(slot, 0)).then_inc(src_in[slot], 16)

            def gather_dst(i, c):
                slot = c % SLOTS
                indirect(x_dst[:, slot, :], None, x[:, :], by(slot, 1)).then_inc(dst_in[slot], 16)

            for c in range(2):
                gather_src(0, c)
                gather_dst(0, c)

            def step(i, c):
                s = SLOTS * i + c
                b = c % 2
                if pool_shares(c, 4):
                    pool.wait_ge(S["dve_m"], s - 3)
                    need(pool, S["pe_c"], s - 5)
                    if is_dense(c, 6):
                        pool.wait_ge(x1_stored[b], 16 * since(i, c, 4 + b, 2))
                    pool.nop(nofuse=True)
                    pool.tensor_scalar(x1[:, b, CH - 1, :], hn[:, (c - 4) % SLOTS, CH - 1, :],
                                       st[:, 7, ROOT - 1:ROOT], st[:, 3, CH - 1:CH], ALU.mult, ALU.add) \
                        .then_inc(S["pool_x"], 1)
                if c == 1:
                    pool.wait_ge(S["vectors_in"], 16 * 3)
                if is_tile(c, 1):
                    pool.wait_ge(S["dve_te"], s)
                    q = pooled[:, b, :]
                    pool.tensor_tensor(q, q, vec_raw[:, BET_P, :], ALU.add).then_inc(S["pool_p"], 1)
                if is_tile(c, -2):
                    slot = (c + 2) % SLOTS
                    need(pool, S["pe_a"], s - 1)
                    if c + 2 >= SLOTS:
                        pool.wait_ge(dst_stored[slot], 16 * since(i, c + 2, slot, SLOTS))
                    gather_src(i, c + 2)
                if is_dense(c, 1):
                    pool.wait_ge(S["dve_t"], s)
                    h = hn[:, (c - 1) % SLOTS, :, :]
                    pool.tensor_tensor(h, h, vec_raw[:, BET_F:BET_F + 1, :].broadcast_to([P, CH, D]),
                                       ALU.add).then_inc(S["pool_b"], 1)
                if is_tile(c, -2):
                    gather_dst(i, c + 2)
                if is_group(c, 4) and not is_dense(c, 4):
                    n = LAST_TILES if c - 4 == GROUPS - 1 else CH
                    if c - 4 == DENSE:
                        pool.wait_ge(S["scat_ready"], 1)
                        for j in range(2):
                            pool.wait_ge(x1_stored[j], 16 * (DENSE // 2))
                    slot, d = c % SLOTS, s - 4 - DENSE
                    fetch((idx[:, slot, 0:n], scat_i[:, bass.ds(d * CH, n)]))
                    pool.wait_ge(S["idx_ready"], 2 * TILES + d + 1)
                    pool.wait_ge(S["act_x"], s - 3)
                    for m in range(n):
                        indirect(x1_table[:, :], by(slot, m), x1[:, b, m, :], None).then_inc(x1_scattered[b], 16)

            run_steps(pool, PLAN_A, step)

            n_even = len([g for g in range(EDGE) if (g + DENSE + 4) % 2 == 0])
            for b, n in ((0, n_even), (1, EDGE - n_even)):
                short = (GROUPS + 3) % 2 == b
                pool.wait_ge(x1_scattered[b], 16 * (n * CH - (CH - LAST_TILES) * short))
            for j in range(2):
                pool.wait_ge(out_stored[j], 16 * (DENSE // 2))
            FETCHED = 2 * TILES + EDGE

            def gather_x1(i, c):
                q, slot = SLOTS * i + c, c % SLOTS
                for n in range(PAIR):
                    indirect(rows[:, slot, n, :], None, x1_table[:, :], by(slot, n)).then_inc(x1_in[slot], 16)

            def fetch_pair(i, c):
                fetch((idx[:, c % SLOTS, 0:PAIR], src_i[:, bass.ds((SLOTS * i + c) * PAIR, PAIR)]))

            for c in range(2):
                fetch_pair(0, c)
                pool.wait_ge(S["idx_ready"], FETCHED + c + 1)
                gather_x1(0, c)

            def step_c(i, c):
                s = SLOTS * i + c
                slot = c % SLOTS
                in_, out_ = c + 2 < PAIRS, 0 <= c - 4 < PAIRS
                fetched = 2 + s + (s - 4 if c >= 4 else 0) if c + 2 <= PAIRS else PAIRS + s - 4
                new = 0
                if in_:
                    need(pool, S["pe_g"], s - 1)
                    fetch_pair(i, c + 2)
                    new += 1
                if out_:
                    pool.wait_ge(S["act_out"], s - 3)
                    fetch((idx[:, slot, PAIR:2 * PAIR], scat_i[:, bass.ds((s - 4) * PAIR, PAIR)]))
                    new += 1
                pool.wait_ge(S["idx_ready"], FETCHED + fetched + new)
                if in_:
                    gather_x1(i, c + 2)
                if out_:
                    for n in range(PAIR):
                        indirect(out[:, :], by(slot, PAIR + n), outb[:, c % 2, PAIR * (c // 2 % 2) + n, :], None) \
                            .then_inc(out_scattered[slot], 16)

            run_steps(pool, PLAN_C, step_c)
            for j in range(SLOTS):
                pool.wait_ge(out_scattered[j], 16 * PAIR * len(range(j, PAIRS, SLOTS)))

        @block.tensor
        def _(pe):
            pe.wait_ge(S["ident_ready"], 1)
            pe.wait_ge(S["const_ready"], N_CONST)

            def step(i, c):
                s = SLOTS * i + c
                slot, b = c % SLOTS, c % 2

                def dense_products(bank, bias_row, w, edge):
                    pe.matmul(bank, ones3[:, :], bias3[:, bias_row, :], start=True, stop=False,
                              skip_group_check=True)
                    for m in range(CH):
                        last = pe.matmul(bank[:, cols(m, m + 1)], xT[:, 1 - b, m, :], w_cen[:, w, :],
                                         start=False, stop=not edge, skip_group_check=True)
                        if edge:
                            last = pe.matmul(bank[:, cols(m, m + 1)], agg_now[:, 1 - b, m, :],
                                             w_cen[:, W_BOT, :], start=False, stop=True, skip_group_check=True)
                    return last

                if c == 1:
                    pe.wait_ge(S["setup_dve"], 1)
                if is_dense(c, 1):
                    pe.wait_ge(S["act_a"], s)
                    need(pe, S["dve_h"], s - 1)
                    dense_products(HD, 0, W_TOP, 0).then_inc(S["pe_b"], 1)
                elif is_group(c, 1):
                    pe.wait_ge(S["act_a"], s)
                    pe.wait_ge(S["dve_h"], DENSE)
                    pe.wait_ge(S["dve_t"], s - 2)
                    dense_products(H[1 - b], 0, W_TOP, True).then_inc(S["pe_b"], 1)
                if is_tile(c, 2):
                    pe.wait_ge(S["pool_p"], s - 1)
                    need(pe, S["dve_scan"], s - 2)
                    pe.transpose(PT, pooled[:, 1 - b, :], ident[:, :]).then_inc(S["pe_cp"], 1)
                if is_tile(c, 1):
                    pe.matmul(HE, xT[:, 1 - b, SRC, :], w_cen[:, W_POOL, :],
                              start=True, stop=True).then_inc(S["pe_e"], 1)
                if is_dense(c, 1):
                    need(pe, S["dve_t"], s - 1)
                    dense_products(HG, 2, W_GAM, 0).then_inc(S["pe_bg"], 1)
                if is_group(c, 0):
                    need(pe, S["act_a"], s)
                    pe.wait_ge(rows_in[slot], 16 * since(i, c + SLOTS, slot, SLOTS))
                    if is_tile(c, 0):
                        pe.wait_ge(src_in[slot], 16 * since(i, c + SLOTS, slot, SLOTS))
                    for m in range(CH + 1 if is_tile(c, 0) else CH):
                        last = pe.transpose(XT[:, cols(m, m + 1)], rows[:, slot, m, :], ident[:, :])
                    last.then_inc(S["pe_a"], 1)
                if c == 5:
                    pe.wait_ge(S["deg_dve"], 4)
                if is_group(c, 5):
                    pe.wait_ge(S["act_x"], s - 4)
                    if pool_shares(c, 5):
                        pe.wait_ge(S["pool_x"], s - 4)
                    need(pe, S["act_c"], s - 5)
                    for m in range(CH):
                        last = pe.transpose(VT[:, cols(m, m + 1)], x1[:, 1 - b, m, :], ident[:, :])
                    last.then_inc(S["pe_c"], 1)
                if is_group(c, 6):
                    pe.wait_ge(S["act_c"], s - 5)
                    need(pe, S["act_o"], s - 7)
                    pe.matmul(Y[b], ones3[:, :], bias3[:, 1, :], start=True, stop=False, skip_group_check=True)
                    for m in range(CH):
                        last = pe.matmul(Y[b][:, cols(m, m + 1)], x1T[:, 1 - b, m, :], w_cen[:, W_ROOT, :],
                                         start=False, stop=True, skip_group_check=True)
                    last.then_inc(S["pe_d"], 1)
                if c in degree_products:
                    degree_products[c]()

            def ends():
                pe.wait_ge(S["deg_dve"], 1)
                pe.matmul(GT[0:1, 0:TILES], seg[:, 1, P - 1:P], ident[0:TILES, 0:TILES], start=True, stop=True)
                pe.matmul(GT[0:1, P:P + TILES], seg[:, 2, P - 1:P], ident[0:TILES, 0:TILES], start=True, stop=True) \
                    .then_inc(S["deg_pe"], 1)

            def carries():
                pe.wait_ge(S["deg_dve"], 2)
                pe.matmul(GT[0:TILES, 0:1], carry[0:1, 2, 0:TILES], one[0:1, 0:1], start=True, stop=True) \
                    .then_inc(S["deg_pe"], 1)

            def to_columns():
                pe.wait_ge(S["deg_dve"], 3)
                pe.transpose(GT[:, 0:TILES], seg[:, 4, :], ident[0:TILES, 0:TILES]).then_inc(S["deg_pe"], 1)

            degree_products = {0: ends, 1: carries, 2: to_columns}
            run_steps(pe, PLAN_A, step)

            pe.wait_ge(S["act_o"], GROUPS)
            pe.wait_ge(S["dve_scan"], TILES)
            pe.wait_ge(S["dve_t"], GROUPS)
            pe.wait_ge(S["onehot"], 2)

            def step_c(i, c):
                s = SLOTS * i + c
                slot, b = c % SLOTS, c % 2
                if 0 <= c - 2 < PAIRS:
                    pe.wait_ge(S["dve_prod"], PAIR * (s - 1))
                    need(pe, S["dve_sum"], s - 4)
                    for m in range(NB):
                        last = pe.matmul(MT[b][:, 0:PAIR * D], w_cen[:, W_BASE + m, :],
                                         prod[:, b, m, :, :].rearrange("p t d -> p (t d)"),
                                         start=(m == 0), stop=(m == NB - 1))
                    last.then_inc(S["pe_m"], 1)
                if c < PAIRS:
                    need(pe, S["act_g"], s)
                    pe.wait_ge(x1_in[slot], 16 * PAIR * since(i, c + SLOTS, slot, SLOTS))
                    for n in range(PAIR):
                        last = pe.transpose(GT[:, cols(n, n + 1)], rows[:, slot, n, :], ident[:, :])
                    last.then_inc(S["pe_g"], 1)

                def coefficients(n):
                    if c < PAIRS:
                        need(pe, S["dve_prod"], PAIR * (s - 1) + n + 1)
                        for m in range(NB):
                            last = pe.matmul(CB[n][:, cols(m, m + 1)], comp_rep[:, m, :],
                                             onehot[:, bass.ds((s * PAIR + n) * P, P)], start=True, stop=True,
                                             skip_group_check=True)
                        last.then_inc(S["pe_cb"], 1)

                coefficients(0)
                if 0 <= c - 3 < PAIRS:
                    pe.wait_ge(S["dve_sum"], s - 2)
                    need(pe, S["dve_y"], s - 3)
                    for n in range(PAIR):
                        last = pe.transpose(ST[:, cols(n, n + 1)], sums[:, 1 - b, n, :], ident[:, :])
                    last.then_inc(S["pe_s"], 1)
                coefficients(1)

            run_steps(pe, PLAN_C, step_c)

        @block.scalar
        def _(act):
            for tile, ap in ((src_i, src_cols), (dst_i, dst_cols)):
                act.dma_start(tile[:, :], ap).then_inc(S["index_in"], 16)
            vectors = (final_b, bias, pool_b, ln_final_g, ln_final_b, ln_pool_g, ln_pool_b)
            for v in (0, 1, GAM_F):
                act.dma_start(vec_raw[:, v, :], vectors[v].broadcast_to([P, D])).then_inc(S["weights_in"], 16)
            act.dma_start(soft[:, 0:1], coeff_raw.broadcast_to([P, 1])).then_inc(S["soft_in"], 16)
            act.dma_start(e_weight[:, :], weight_cols).then_inc(S["soft_in"], 16)
            for v in (GAM_P, BET_P, BET_F):
                act.dma_start(vec_raw[:, v, :], vectors[v].broadcast_to([P, D])).then_inc(S["vectors_in"], 16)
            act.dma_start(dst_n[:, :], dst_next_cols).then_inc(S["edges_in"], 16)
            for k in range(PARTS):
                act.dma_start(comp_raw[k * REL:(k + 1) * REL, :], comp).then_inc(S["edges_in"], 16)
            act.wait_ge(S["soft_dve"], 1)
            nc.scalar.activation(soft[:, 2:3], soft[:, 1:2], ACT.Exp, scale=-1.0).then_inc(S["soft_act"], 1)
            act.wait_ge(S["soft_act"], 1)
            nc.scalar.activation(soft[:, 3:4], soft[:, 2:3], ACT.Ln, bias=1.0).then_inc(S["soft_act"], 1)
            nc.scalar.activation(soft[:, 6:7], soft[:, 2:3], ACT.Sqrt)

            def step(i, c):
                s = SLOTS * i + c
                b = c % 2
                if is_group(c, 0):
                    act.wait_ge(S["pe_a"], s + 1)
                    need(act, S["pe_b"], s - 1)
                    if is_dense(c, 2):
                        act.wait_ge(S["pe_bg"], s - 1)
                    n = CH + 1 if is_tile(c, 0) else CH
                    if not is_dense(c, 0):
                        act.wait_ge(S["dve_scan"], TILES - 2 if c < DENSE + 2 else TILES)
                        nc.scalar.copy(agg_now[:, b, :, :], agg_all[:, bass.ds((s - DENSE) * CH, CH), :])
                    nc.scalar.copy(xT[:, b, 0:n, :].rearrange("p c d -> p (c d)"), XT[:, cols(0, n)]) \
                        .then_inc(S["act_a"], 1)
                if 1 <= c <= GROUPS + 3:
                    act.wait_ge(S["dve_q"], s)
                    if is_group(c, 5):
                        act.wait_ge(S["act_x"], s - 4)
                    if pool_shares(c, 5):
                        act.wait_ge(S["pool_x"], s - 4)
                    if is_group(c, 8):
                        act.wait_ge(S["act_o"], s - 7)
                    nc.scalar.activation(st[:, 7, :], st[:, 6, :], ACT.Sqrt).then_inc(S["act_q"], 1)
                if is_group(c, 5):
                    act.wait_ge(S["pe_c"], s - 4)
                    need(act, S["pe_d"], s - 6)
                    nc.scalar.copy(x1T[:, b, :, :].rearrange("p c d -> p (c d)"), VT).then_inc(S["act_c"], 1)
                if is_group(c, 4):
                    act.wait_ge(S["dve_m"], s - 3)
                    need(act, S["pe_c"], s - 5)
                    if is_dense(c, 6):
                        act.wait_ge(x1_stored[b], 16 * since(i, c, 4 + b, 2))
                    elif is_group(c, 6):
                        act.wait_ge(x1_scattered[b], 16 * CH * since(i, c, DENSE + 4 + (b + DENSE + 4) % 2, 2))
                    for m in range(CH - pool_shares(c, 4)):
                        last = nc.scalar.activation(x1[:, b, m, :], hn[:, (c - 4) % SLOTS, m, :], ACT.Identity,
                                                    bias=st[:, 3, m:m + 1], scale=st[:, 7, RES + m:RES + m + 1])
                    last.then_inc(S["act_x"], 1)
                if is_dense(c, 6):
                    act.wait_ge(S["pe_d"], s - 5)
                    need(act, S["dve_q"], s - 1)
                    for m in range(CH):
                        last = nc.scalar.activation(junk[:, b, m, :], Y[b][:, cols(m, m + 1)], ACT.Square,
                                                    accum_out=ysq[:, b, m:m + 1])
                    last.then_inc(S["act_y"], 1)
                if is_dense(c, 7):
                    act.wait_ge(S["act_q"], s)
                    if c >= 9:
                        act.wait_ge(out_stored[b], 16 * since(i, c, 8 - b, 2))
                    for m in range(CH):
                        last = nc.scalar.activation(outb[:, b, m, :], Y[1 - b][:, cols(m, m + 1)], ACT.Copy,
                                                    scale=st[:, 7, ROOT + m:ROOT + m + 1])
                    last.then_inc(S["act_o"], 1)
                elif is_group(c, 7):
                    act.wait_ge(S["pe_d"], s - 6)
                    nc.scalar.copy(y_root[:, bass.ds((s - 7 - DENSE) * CH * D, CH * D)], Y[1 - b]) \
                        .then_inc(S["act_o"], 1)

            run_steps(act, PLAN_A, step)

            def step_c(i, c):
                s = SLOTS * i + c
                b = c % 2
                if c < PAIRS:
                    act.wait_ge(S["pe_g"], s + 1)
                    need(act, S["dve_prod"], PAIR * (s - 1))
                    nc.scalar.copy(xT[:, b, 0:PAIR, :].rearrange("p c d -> p (c d)"), GT[:, 0:PAIR * D]) \
                        .then_inc(S["act_g"], 1)
                if 0 <= c - 4 < PAIRS:
                    act.wait_ge(S["dve_r"], s - 3)
                    need(act, S["act_out"], s - 4)
                    nc.scalar.activation(st[:, 7, 0:PAIR], st[:, 6, 0:PAIR], ACT.Sqrt).then_inc(S["act_r"], 1)
                    act.wait_ge(S["act_r"], s - 3)
                    if c >= 8:
                        act.wait_ge(out_scattered[c % SLOTS], 16 * PAIR * since(i, c, 4 + c % SLOTS, SLOTS))
                    for n in range(PAIR):
                        last = nc.scalar.activation(outb[:, b, PAIR * (c // 2 % 2) + n, :], y_rows[:, b, n, :],
                                                    ACT.Copy, scale=st[:, 7, n:n + 1])
                    last.then_inc(S["act_out"], 1)

            run_steps(act, PLAN_C, step_c)

        @block.vector
        def _(dve):
            own = Chain(dve, S["dve_own"])

            own.mark(dve.memset(bn[:, :, :], 0.0))
            own.mark(dve.memset(ysq[:, :, :], 0.0))
            own.mark(dve.memset(st[:, :, :], 0.0))

            def centre(to, of, mean):
                n = to.shape[1]
                own.link(dve.tensor_reduce(mean, of, AX_X, ALU.add))
                own.link(dve.tensor_scalar(mean, mean, 1.0 / D, None, ALU.mult))
                own.mark(dve.tensor_tensor(to, of, mean.unsqueeze(2).broadcast_to([P, n, D]), ALU.subtract))

            dve.wait_ge(S["const_ready"], N_CONST)
            for k in range(PARTS):
                own.mark(dve.tensor_scalar(part_mask[:, 0, k:k + 1], part_id[:, :], float(k), None, ALU.is_equal))
            own.mark(dve.tensor_scalar(part_mask[:, 1, 0:1], part_id[:, :], float(REL), None, ALU.is_lt))
            own.mark(dve.tensor_scalar(part_mask[:, 1, 2:3], part_id[:, :], float(2 * REL), None, ALU.is_ge))
            own.link(dve.tensor_scalar(part_mask[:, 1, 1:2], part_id[:, :], float(REL), None, ALU.is_ge))
            own.mark(dve.tensor_tensor(part_mask[:, 1, 1:2], part_mask[:, 1, 1:2], part_mask[:, 1, 2:3],
                                       ALU.subtract))

            def split3(value, parts, rem, masks, n):
                own.link(dve.tensor_copy(parts[0], value))
                own.link(dve.tensor_tensor(rem[0], value, parts[0], ALU.subtract))
                own.link(dve.tensor_copy(parts[1], rem[0]))
                own.link(dve.tensor_tensor(rem[1], rem[0], parts[1], ALU.subtract))
                own.link(dve.tensor_copy(parts[2], rem[1]))
                own.link(dve.tensor_scalar(rem[0], parts[0], masks[0:n, 0:1], None, ALU.mult))
                for k in range(1, PARTS):
                    own.link(dve.scalar_tensor_tensor(rem[0], parts[k], masks[0:n, k:k + 1], rem[0],
                                                      ALU.mult, ALU.add))

            same, pos, run, deg = (seg[:, k, :] for k in (0, 1, 2, 3))
            dve.wait_ge(S["rows_of_dst_in"], 16 * 2)
            dve.tensor_tensor(same_rows[:, :], d_cur[:, :], d_prev[:, :], ALU.is_equal).then_inc(S["mask_made"], 1)
            own.link(dve.tensor_tensor(same, d_cur[:, :], d_prev[:, :], ALU.is_equal))
            own.mark(dve.tensor_tensor_scan(run, same, same, 1.0, ALU.mult, ALU.min))
            own.link(dve.tensor_copy(deg, same))
            own.link(dve.memset(deg[:, 0:1], 0.0))
            dve.tensor_tensor_scan(pos, deg, deg, 0.0, ALU.mult, ALU.add).then_inc(S["deg_dve"], 1)

            dve.wait_ge(S["weights_in"], 16 * 8)
            dve.wait_ge(S["soft_in"], 16 * 2)
            own.link(dve.tensor_scalar(soft[:, 4:5], soft[:, 0:1], -1.0, None, ALU.mult))
            dve.tensor_tensor(soft[:, 1:2], soft[:, 0:1], soft[:, 4:5], ALU.max).then_inc(S["soft_dve"], 1)
            dve.wait_ge(S["ident_ready"], 1)
            own.mark(dve.tensor_tensor(w_raw[:, W_ROOT, :], w_raw[:, W_ROOT, :], ident[:, :], ALU.add))
            centre(vec_cen[:, :, :], vec_raw[:, 0:3, :], row_mean[:, 12:15])
            centre(w_cen[:, 0:W_BASE, :], w_raw[:, 0:W_BASE, :], row_mean[:, 0:W_BASE])
            own.link(dve.tensor_copy(biases[:, 0:2, :], vec_cen[0:PARTS, 0:2, :]))
            own.mark(dve.tensor_tensor(biases[:, 2, :], vec_cen[0:PARTS, 0, :], vec_raw[0:PARTS, GAM_F, :], ALU.mult))
            own.link(dve.tensor_tensor(w_cen[:, W_GAM, :], w_cen[:, W_TOP, :], vec_raw[:, GAM_F, :], ALU.mult))
            parts = [split[:, k * 3 * D:(k + 1) * 3 * D].rearrange("p (v d) -> p v d", v=3) for k in range(PARTS)]
            split3(biases, parts, [rest[:, 0:3, :], work[0:PARTS, 12:15, :]], part_mask[:, 0, :], PARTS)
            for v in range(3):
                last = dve.tensor_copy(bias3[:, v, :].rearrange("p (c d) -> p c d", c=CH),
                                       rest[:, v:v + 1, :].broadcast_to([PARTS, CH, D]))
                own.mark(last) if v < 2 else last.then_inc(S["setup_dve"], 1)
            dve.wait_ge(S["soft_act"], 2)
            own.link(dve.tensor_scalar(soft[:, 5:6], soft[:, 0:1], 0.0, soft[:, 3:4], ALU.max, ALU.add))
            own.link(dve.tensor_scalar(e_scale[:, :], e_weight[:, :], soft[:, 5:6], 1.0, ALU.mult, ALU.add))

            K3 = PARTS * REL

            def tile_ends():
                dve.wait_ge(S["deg_pe"], 1)
                own.mark(dve.tensor_scalar(carry[:, 0, 0:TILES], GT[0:1, 0:TILES], 1.0, None, ALU.add))
                own.link(dve.tensor_copy(carry[:, 1, 0:TILES], GT[0:1, P:P + TILES]))
                dve.tensor_tensor_scan(carry[:, 2, 1:TILES], carry[:, 1, 0:TILES - 1], carry[:, 0, 0:TILES - 1], 0.0,
                                       ALU.mult, ALU.add).then_inc(S["deg_dve"], 1)

            def inverse_degrees():
                dve.wait_ge(S["deg_pe"], 2)
                own.link(dve.tensor_copy(carry_col[:, :], GT[0:TILES, 0:1]))
                own.link(dve.scalar_tensor_tensor(pos, run, carry_col[:, 0:1], pos, ALU.mult, ALU.add))
                own.link(dve.tensor_scalar(deg, pos, 1.0, None, ALU.add))
                dve.reciprocal(seg[:, 4, :], deg).then_inc(S["deg_dve"], 1)

            def degree_columns():
                dve.wait_ge(S["deg_pe"], 3)
                dve.tensor_copy(inv_deg[:, :], GT[:, 0:TILES]).then_inc(S["deg_dve"], 1)
                dve.wait_ge(S["index_in"], 16 * 2)
                dve.wait_ge(S["edges_in"], 16 * (1 + PARTS))
                own.link(dve.tensor_tensor(same_next[:, :], dst_i[:, :], dst_n[:, :], ALU.is_equal))
                dve.scalar_tensor_tensor(scat_i[:, :], same_next[:, :], float(SKIP), dst_i[:, :],
                                         ALU.mult, ALU.add).then_inc(S["scat_ready"], 1)

            def bases():
                dve.wait_ge(S["bases_in"], 16)
                centre(w_cen[:, W_BASE:W_BASE + NB, :], w_raw[:, W_BASE:W_BASE + NB, :], row_mean[:, 4:4 + NB])

            def basis_coefficients():
                split3(comp_raw[:, :], [comp_split[:, k, :] for k in range(PARTS)],
                       [comp_rest[:, k, :] for k in range(2)], part_mask[:, 1, :], K3)
                own.link(dve.tensor_copy(comp_rep[:, :, :], comp_rest[:, 0, :].unsqueeze(2).broadcast_to([K3, NB, P])))
                own.link(dve.tensor_scalar(rel_id[:, :], part_mask[0:K3, 1, 1:2], -float(REL), part_id[0:K3, :],
                                           ALU.mult, ALU.add))
                own.link(dve.scalar_tensor_tensor(rel_id[:, :], part_mask[0:K3, 1, 2:3], -float(2 * REL),
                                                  rel_id[:, :], ALU.mult, ALU.add))

            def one_hot(a, z, loads):
                dve.wait_ge(S["types_in"], 16 * loads)
                dve.tensor_scalar(onehot[:, a:z], types[0:K3, a:z], rel_id[:, 0:1], None,
                                  ALU.is_equal).then_inc(S["onehot"], 1)

            beside = {0: tile_ends, 1: inverse_degrees, 2: degree_columns, GROUPS + 3: basis_coefficients}

            def moments(a, b):
                me, m2e, mo, m2o = (bn[:, a:b, k] for k in (1, 2, 4, 5))
                at = own.mark(dve.tensor_tensor(st[:, 0, a:b], me, mo, ALU.subtract))
                own.mark(dve.scalar_tensor_tensor(st[:, 1, a:b], m2e, D * LN_EPS, m2o, ALU.add, ALU.add))
                return at

            def spread(a, b):
                return own.mark(dve.scalar_tensor_tensor(st[:, 2, a:b], st[:, 0, a:b], 0.25, st[:, 0, a:b],
                                                         ALU.mult, ALU.mult))

            def variance(a, b):
                return own.mark(dve.scalar_tensor_tensor(st[:, 5, a:b], st[:, 1, a:b], 1.0 / D, st[:, 2, a:b],
                                                         ALU.mult, ALU.add))

            bases()
            dve.wait_ge(S["vectors_in"], 16 * 3)

            def step(i, c):
                s = SLOTS * i + c
                b = c % 2
                if is_group(c, 1):
                    dve.wait_ge(S["pe_b"], s)
                    bank = HD if is_dense(c, 1) else H[1 - b]
                    for m in range(CH):
                        last = own.mark(dve.bn_stats(bn[:, m, :], bank[:, cols(m, m + 1)])) if m < CH - 1 \
                            else dve.bn_stats(bn[:, m, :], bank[:, cols(m, m + 1)]).then_inc(S["dve_h"], 1)
                if is_tile(c, 1):
                    dve.wait_ge(S["pe_e"], s)
                    hp_at = own.mark(dve.scalar_tensor_tensor(hp[:, :], HE, e_scale[:, bass.ds(s - 1, 1)],
                                                              vec_cen[:, 2, :], ALU.mult, ALU.add))
                if is_tile(c, 2):
                    if c == 2:
                        dve.wait_ge(S["masks_in"], 16)
                    dve.wait_ge(S["pe_cp"], s - 1)
                    need(dve, S["dve_scan"], s - 2)
                    first = 0.0 if c == 2 else agg_line[:, bass.ds((s - 2) * P - 1, 1)]
                    dve.tensor_tensor_scan(agg_line[:, bass.ds((s - 2) * P, P)], same_prev[:, bass.ds((s - 2) * P, P)],
                                           PT, first, ALU.mult, ALU.max).then_inc(S["dve_scan"], 1)
                if is_tile(c, 1):
                    own.need(hp_at)
                    own.mark(dve.bn_stats(bn[:, SRC, :], hp[:, :]))

                def residual_sum():
                    h = hn[:, (c - 2) % SLOTS, :, :].rearrange("p c d -> p (c d)")
                    dve.scalar_tensor_tensor(
                        h, h, 0.0, rows[:, (c - 2) % SLOTS, 0:CH, :].rearrange("p c d -> p (c d)"),
                        ALU.max, ALU.add).then_inc(S["dve_v"], 1)

                stats_at = own.count
                if is_group(c, 2) and not is_dense(c, 2):
                    h = hn[:, (c - 2) % SLOTS, :, :]
                    dve.wait_ge(S["dve_t"], s - 1)
                    beta_at = own.mark(dve.tensor_tensor(
                        h, h, vec_raw[:, BET_F:BET_F + 1, :].broadcast_to([P, CH, D]), ALU.add))

                def residual_stats(a, z):
                    if is_group(c, 3):
                        if a == 0:
                            own.need(before_residual)
                            dve.wait_ge(S["dve_v"], s - 2)
                        for m in range(a, z):
                            own.mark(dve.bn_stats(bn[:, RES + m, :], hn[:, (c - 3) % SLOTS, m, :]))

                if 1 <= c <= GROUPS + 3:
                    own.need(stats_at)
                    if is_group(c, 1):
                        dve.wait_ge(S["dve_h"], s)
                    at = moments(0, ROOT)
                    if is_group(c, 4):
                        need(dve, S["dve_m"], s - 4)
                        own.mark(dve.tensor_tensor(st[:, 3, RES:ROOT], bn[:, RES:ROOT, 1], bn[:, RES:ROOT, 4],
                                                   ALU.add))
                    before_residual = own.count
                    own.need(at)
                    at = spread(0, ROOT)
                    if is_dense(c, 7):
                        dve.wait_ge(S["act_y"], s - 6)
                        own.mark(dve.tensor_scalar(st[:, 5, ROOT:ROOT + CH], ysq[:, 1 - b, :], 1.0 / D, LN_EPS,
                                                   ALU.mult, ALU.add))
                    residual_stats(0, 1)
                    own.need(at)
                    at = variance(0, ROOT)
                    residual_stats(1, 2)
                    own.need(at)
                    n = ROOT + CH if is_dense(c, 7) else ROOT
                    dve.reciprocal(st[:, 6, 0:n], st[:, 5, 0:n]).then_inc(S["dve_q"], 1)
                residual_stats(2, CH)
                if 1 <= c <= GROUPS + 3:
                    dve.wait_ge(S["act_q"], s)
                if is_group(c, 4):
                    dve.scalar_tensor_tensor(st[:, 3, 0:CH], st[:, 3, RES:ROOT], -0.5, st[:, 7, RES:ROOT],
                                             ALU.mult, ALU.mult).then_inc(S["dve_m"], 1)
                if is_tile(c, 1):
                    need(dve, S["pe_cp"], s - 2)
                    dve.scalar_tensor_tensor(pooled[:, b, :], hp[:, :], st[:, 7, SRC:SRC + 1],
                                             vec_raw[:, GAM_P, :], ALU.mult, ALU.mult).then_inc(S["dve_te"], 1)
                if is_group(c, 2):
                    if is_dense(c, 2):
                        dve.wait_ge(S["pool_b"], s - 1)
                    else:
                        own.need(beta_at)
                    residual_sum()
                if is_group(c, 1):
                    need(dve, S["act_x"], s - 4)
                    if is_dense(c, 1):
                        dve.wait_ge(S["pe_bg"], s)
                        last = dve.tensor_tensor(
                            hn[:, (c - 1) % SLOTS, :, :], HG.rearrange("p (c d) -> p c d", c=CH),
                            st[:, 7, 0:CH].unsqueeze(2).broadcast_to([P, CH, D]), ALU.mult)
                    for m in range(0 if is_dense(c, 1) else CH):
                        last = dve.scalar_tensor_tensor(hn[:, (c - 1) % SLOTS, m, :], H[1 - b][:, cols(m, m + 1)],
                                                        st[:, 7, m:m + 1], vec_raw[:, GAM_F, :],
                                                        ALU.mult, ALU.mult)
                        if m < CH - 1:
                            own.mark(last)
                    last.then_inc(S["dve_t"], 1)
                if c in beside:
                    beside[c]()

            run_steps(dve, PLAN_A, step, own, (15, 16))

            one_hot(0, EARLY, 1)
            one_hot(EARLY, EP, 2)
            own = Chain(dve, S["c_own"])

            def step_c(i, c):
                s = SLOTS * i + c
                b = c % 2
                last_pair = 0 <= c - 4 < PAIRS

                def product(n):
                    if 0 <= c - 1 < PAIRS:
                        dve.wait_ge(S["pe_cb"], PAIR * (s - 1) + n + 1)
                        if n == 0:
                            dve.wait_ge(S["act_g"], s)
                            need(dve, S["pe_m"], s - 3)
                        dve.tensor_tensor(prod[:, 1 - b, :, n, :], CB[n].rearrange("p (m d) -> p m d", m=NB),
                                          xT[:, 1 - b, n:n + 1, :].broadcast_to([P, NB, D]), ALU.mult) \
                           .then_inc(S["dve_prod"], 1)

                if last_pair:
                    dve.wait_ge(S["pe_s"], s - 3)
                    need(dve, S["act_out"], s - 5)
                    for n in range(PAIR):
                        t = (s - 4) * PAIR + n
                        last = dve.scalar_tensor_tensor(y_rows[:, b, n, :], ST[:, cols(n, n + 1)],
                                                        inv_deg[:, bass.ds(t, 1)], y_root[:, bass.ds(t * D, D)],
                                                        ALU.mult, ALU.add)
                    last.then_inc(S["dve_y"], 1)
                    dve.wait_ge(S["dve_y"], s - 3)
                    for n in range(PAIR):
                        at = own.mark(dve.bn_stats(bn[:, n, :], y_rows[:, b, n, :]))
                product(0)
                if last_pair:
                    own.need(at)
                    at = moments(0, PAIR)
                if 0 <= c - 3 < PAIRS:
                    dve.wait_ge(S["pe_m"], s - 2)
                    need(dve, S["pe_s"], s - 4)
                    need(dve, S["dve_sum"], s - 3)
                    first = 0.0 if c == 3 else sums[:, b, PAIR - 1, D - 1:D]
                    dve.tensor_tensor_scan(sums[:, 1 - b, :, :].rearrange("p t d -> p (t d)"),
                                           same_prev[:, bass.ds((s - 3) * PAIR * P, PAIR * P)],
                                           MT[1 - b][:, 0:PAIR * D], first, ALU.mult, ALU.add) \
                       .then_inc(S["dve_sum"], 1)
                if last_pair:
                    own.need(at)
                    at = spread(0, PAIR)
                product(1)
                if last_pair:
                    own.need(at)
                    own.need(variance(0, PAIR))
                    need(dve, S["act_r"], s - 4)
                    dve.reciprocal(st[:, 6, 0:PAIR], st[:, 5, 0:PAIR]).then_inc(S["dve_r"], 1)

            run_steps(dve, PLAN_C, step_c, own, (6,))


def kernel(x, src, dst, edge_type_16, edge_weight, L0_gnn_pool_w, L0_gnn_pool_b, L0_gnn_ln_pool_g,
           L0_gnn_ln_pool_b, L0_gnn_final_w, L0_gnn_final_b, L0_gnn_ln_final_g, L0_gnn_ln_final_b,
           L0_gnn_coeff_raw, L1_gnn_weight, L1_gnn_comp, L1_gnn_bias):
    import numpy as np
    import concourse.bacc as bacc
    from concourse.bass_utils import run_bass_kernel_spmd

    x, src, dst, edge_type, edge_weight = (np.asarray(a) for a in (x, src, dst, edge_type_16, edge_weight))
    N, E = x.shape[0], src.shape[0]
    tiles = -(-E // P)

    def line(a, fill, extra=0):
        return np.concatenate([a, np.full(tiles * P + extra - E, fill, a.dtype)])

    def by_tile(a):
        return np.ascontiguousarray(a.reshape(tiles, P).T)

    dst_ext = line(dst, N, 1)
    arrays = {
        "x": x,
        "src_cols": by_tile(line(src, 0)),
        "dst_cols": by_tile(dst_ext[:-1]),
        "dst_next_cols": by_tile(dst_ext[1:]),
        "dst_rows": dst_ext[:-1].reshape(tiles, P),
        "dst_prev_rows": np.concatenate([np.full(1, -1, dst.dtype), dst_ext[:-2]]).reshape(tiles, P),
        "type_line": line(edge_type, 0)[None, :],
        "weight_cols": by_tile(line(edge_weight, 0)),
        "pool_w": L0_gnn_pool_w, "pool_b": L0_gnn_pool_b, "ln_pool_g": L0_gnn_ln_pool_g,
        "ln_pool_b": L0_gnn_ln_pool_b, "final_w": L0_gnn_final_w, "final_b": L0_gnn_final_b,
        "ln_final_g": L0_gnn_ln_final_g, "ln_final_b": L0_gnn_ln_final_b, "coeff_raw": L0_gnn_coeff_raw,
        "weight": L1_gnn_weight, "comp": L1_gnn_comp, "bias": L1_gnn_bias,
    }
    nc = bacc.Bacc("TRN2", target_bir_lowering=False, num_devices=1)
    feed, aps = {}, {}
    for name, a in arrays.items():
        a = np.asarray(a)
        a = np.ascontiguousarray(a.reshape(1, -1) if a.ndim < 2 else a)
        feed[f"in_{name}"] = a
        aps[name] = nc.dram_tensor(f"in_{name}", a.shape, mybir.dt.from_np(a.dtype), kind="ExternalInput").ap()
    aps["out"] = nc.dram_tensor("out_rows", x.shape, F32, kind="ExternalOutput").ap()
    gnn_kernel(nc, **aps)
    r = run_bass_kernel_spmd(nc, [feed], core_ids=[0])
    return r.results[0]["out_rows"]
```
